# Optimizing a Trainium2 kernel written in Bass

```python
import numpy as np
import jax
import jax.numpy as jnp

def _softmax(x, axis=-1):
    return jax.nn.softmax(x, axis=axis)

def _gelu(x):
    return jax.nn.gelu(x, approximate=True)

def _silu(x):
    return jax.nn.silu(x)

def _sigmoid(x):
    return jax.nn.sigmoid(x)

def _layernorm(x, axis=-1, eps=1e-05):
    m = jnp.mean(x, axis=axis, keepdims=True)
    v = jnp.var(x, axis=axis, keepdims=True)
    return (x - m) / jnp.sqrt(v + eps)

def _scatter_add(tgt, idx, src, axis=0):
    return tgt.at[idx].add(src)

def _segment_sum(src, seg, n):
    return jax.ops.segment_sum(src, seg, n)
kernel_name = 'mk_recurrent_d1_jaxref_r4_87cc1a'

def setup_inputs(seed: int=0):
    np.random.seed(seed)
    _w = jnp.asarray

    def _L0_attn_setup():
        import jax, jax.numpy as jnp
        import numpy as np
        H = 512
        Q_RANK = 64
        SCALE = float(np.sqrt(Q_RANK))
        key = jax.random.key(seed)
        k_x, k_s, k_a, k_o, k_b = jax.random.split(key, 5)
        B, L = (4, 1024)
        x = jax.random.normal(k_x, (B, L, H), dtype=jnp.float32)
        Ws = jax.random.normal(k_s, (H, Q_RANK), dtype=jnp.float32) / np.sqrt(H)
        Wa = jax.random.normal(k_a, (H, Q_RANK), dtype=jnp.float32) / np.sqrt(H)
        Wo = jax.random.normal(k_o, (H, H), dtype=jnp.float32) / np.sqrt(H)
        bo = jax.random.normal(k_b, (H,), dtype=jnp.float32) * 0.01
        return {'x': x, 'Ws': Ws, 'Wa': Wa, 'Wo': Wo, 'bo': bo}
    _L0_attn_in = _L0_attn_setup()

    def _L0_ffn_setup():
        import jax, jax.numpy as jnp
        import numpy as np
        _FP4_LUT = jnp.array([0.0, 0.5, 1.0, 1.5, 2.0, 3.0, 4.0, 6.0, -0.0, -0.5, -1.0, -1.5, -2.0, -3.0, -4.0, -6.0], dtype=jnp.float32)
        GROUP_SIZE = 128
        EPS = 1e-06

        def _dequant_fp4(packed_i32, scales_f16, group_size):
            out_f, in_p = packed_i32.shape
            w = packed_i32.astype(jnp.uint32)
            shifts = jnp.arange(8, dtype=jnp.uint32) * 4
            nib = w[:, :, None] >> shifts & jnp.uint32(15)
            vals = _FP4_LUT[nib.astype(jnp.int32)].reshape(out_f, in_p * 8)
            s = scales_f16.astype(jnp.float32).T
            s_full = jnp.repeat(s, group_size, axis=1)
            return vals * s_full
        key = jax.random.key(seed)
        k1, k2, k3, k4, k5 = jax.random.split(key, 5)
        B, S, H, I = (4, 512, 512, 1408)
        x = jax.random.normal(k1, (B, S, H), dtype=jnp.float32)
        gate_up_packed = jax.random.randint(k2, (2 * I, H // 8), 0, 2147483647, dtype=jnp.int32)
        gate_up_scales = jax.random.uniform(k3, (H // GROUP_SIZE, 2 * I), dtype=jnp.float32).astype(jnp.float16)
        down_packed = jax.random.randint(k4, (H, I // 8), 0, 2147483647, dtype=jnp.int32)
        down_scales = jax.random.uniform(k5, (I // GROUP_SIZE, H), dtype=jnp.float32).astype(jnp.float16)
        return {'x': x, 'gate_up_packed': gate_up_packed, 'gate_up_scales': gate_up_scales, 'down_packed': down_packed, 'down_scales': down_scales}
    _L0_ffn_in = _L0_ffn_setup()
    _d = {'L0_attn_x': _L0_attn_in['x'], 'L0_attn_Ws': _L0_attn_in['Ws'], 'L0_attn_Wa': _L0_attn_in['Wa'], 'L0_attn_Wo': _L0_attn_in['Wo'], 'L0_attn_bo': _L0_attn_in['bo'], 'L0_ffn_gate_up_packed': _L0_ffn_in['gate_up_packed'], 'L0_ffn_gate_up_scales': _L0_ffn_in['gate_up_scales'], 'L0_ffn_down_packed': _L0_ffn_in['down_packed'], 'L0_ffn_down_scales': _L0_ffn_in['down_scales']}
    _x0 = _d['L0_attn_x']
    _d['L0_attn_x'] = jax.random.normal(jax.random.fold_in(jax.random.key(seed), 1), (16, 512, 512), dtype=_x0.dtype)
    del _x0
    return _d

def reference(L0_attn_x, L0_attn_Ws, L0_attn_Wa, L0_attn_Wo, L0_attn_bo, L0_ffn_gate_up_packed, L0_ffn_gate_up_scales, L0_ffn_down_packed, L0_ffn_down_scales):

    def _L0_attn_ref(x, Ws, Wa, Wo, bo):
        import jax, jax.numpy as jnp
        import numpy as np
        H = 512
        Q_RANK = 64
        SCALE = float(np.sqrt(Q_RANK))
        B, L, _ = x.shape
        state = jnp.einsum('blh,hr->blr', x, Ws)
        action = jnp.einsum('blh,hr->blr', x, Wa)
        q_values = jnp.einsum('bir,bjr->bij', state, action) / SCALE
        causal = jnp.tril(jnp.ones((L, L), dtype=bool))
        q_values = jnp.where(causal, q_values, -jnp.inf)
        weights = jax.nn.softmax(q_values, axis=-1)
        out = jnp.einsum('bij,bjh->bih', weights, x)
        return jnp.einsum('bih,ho->bio', out, Wo.T) + bo

    def _L0_ffn_ref(x, gate_up_packed, gate_up_scales, down_packed, down_scales):
        import jax, jax.numpy as jnp
        import numpy as np
        _FP4_LUT = jnp.array([0.0, 0.5, 1.0, 1.5, 2.0, 3.0, 4.0, 6.0, -0.0, -0.5, -1.0, -1.5, -2.0, -3.0, -4.0, -6.0], dtype=jnp.float32)
        GROUP_SIZE = 128
        EPS = 1e-06

        def _dequant_fp4(packed_i32, scales_f16, group_size):
            out_f, in_p = packed_i32.shape
            w = packed_i32.astype(jnp.uint32)
            shifts = jnp.arange(8, dtype=jnp.uint32) * 4
            nib = w[:, :, None] >> shifts & jnp.uint32(15)
            vals = _FP4_LUT[nib.astype(jnp.int32)].reshape(out_f, in_p * 8)
            s = scales_f16.astype(jnp.float32).T
            s_full = jnp.repeat(s, group_size, axis=1)
            return vals * s_full
        I = gate_up_packed.shape[0] // 2
        w_gu = _dequant_fp4(gate_up_packed, gate_up_scales, GROUP_SIZE)
        w_down = _dequant_fp4(down_packed, down_scales, GROUP_SIZE)
        gate_up = jnp.einsum('bsh,oh->bso', x, w_gu)
        gate, up = (gate_up[..., :I], gate_up[..., I:])
        h = jax.nn.silu(gate) * up
        y = jnp.einsum('bsi,hi->bsh', h, w_down)
        rms = jnp.sqrt(jnp.mean(y * y, axis=-1, keepdims=True) + EPS)
        return y / rms
    x = L0_attn_x
    xn = _layernorm(x, axis=-1)
    s = _L0_attn_ref(xn, L0_attn_Ws, L0_attn_Wa, L0_attn_Wo, L0_attn_bo)
    g = _silu(_L0_ffn_ref(xn, L0_ffn_gate_up_packed, L0_ffn_gate_up_scales, L0_ffn_down_packed, L0_ffn_down_scales))
    x = x + s * g
    return x

_drawn_inputs = setup_inputs


def setup_inputs(seed=0):
    import zlib

    import numpy as np

    out = dict(_drawn_inputs(seed))
    spreads = {}
    factors = {'L0_attn_bo': 8.0}
    for name, (base, spread) in spreads.items():
        noise = np.random.default_rng([zlib.crc32(name.encode()), seed]).standard_normal(out[name].shape)
        drawn = base * np.exp(spread * noise) if base else spread * noise
        out[name] = jnp.asarray(drawn.astype(out[name].dtype))
    for name, factor in factors.items():
        out[name] = (out[name] * factor).astype(out[name].dtype)
    return out
```

```python
from contextlib import ExitStack

import concourse.bass as bass
from concourse import mybir

F32 = mybir.dt.float32
F32R = mybir.dt.float32r
F16 = mybir.dt.float16
BF16 = mybir.dt.bfloat16
U16 = mybir.dt.uint16
U32 = mybir.dt.int32
ALU = mybir.AluOpType
ACT = mybir.ActivationFunctionType
AX = mybir.AxisListType

AUX_SLOTS = [("SA", 0), ("V", 0), ("V", 1), ("E", 0), ("V", 2), ("E", 1), ("F", 0), ("V", 3), ("G", 0), ("F", 1),
             ("E", 2), ("G", 1), ("F", 2), ("E", 3), ("G", 2), ("T", 0), ("F", 3), ("T", 1), ("G", 3), ("T", 2),
             ("T", 3), None]


def gated_attention_ffn(nc, x, Ws, Wa, Wo, bo, gu_packed, gu_scales, down_packed, down_scales, out):
    BATCH, SEQ, HID = x.shape
    RANK = Ws.shape[1]
    INNER = gu_packed.shape[0] // 2
    P = 128
    TT = SEQ // P
    KT = HID // P
    STEPS = INNER // P
    UNITS = 2 * KT
    NU = UNITS * STEPS
    QSCALE = float(RANK) ** -0.5
    XSCALE = 1024.0
    LN_EPS, RMS_EPS = 1e-5, 1e-6
    NEG = -3.0e38
    WORDS = HID // 8
    DWORDS = INNER // 8

    x_v = x.rearrange("b (t p) h -> b p t h", p=P)
    out_v = out.rearrange("b (t p) h -> b p t h", p=P)

    ctx = ExitStack()
    with ctx:
        def sb(name, shape, dt):
            return ctx.enter_context(nc.sbuf_tensor(name, shape, dt))

        def pb(name, shape, dt):
            return ctx.enter_context(nc.psum_tensor(name, shape, dt))

        def sem(name):
            return ctx.enter_context(nc.semaphore(name))

        w_gu = sb("w_gu", [P, KT, 2 * INNER], F16)
        wd_hi = sb("wd_hi", [P, STEPS, HID], F32R)
        wd_lo = sb("wd_lo", [P, STEPS, HID], BF16)
        wo_hi = sb("wo_hi", [P, KT, HID], F32R)
        wo_lo = sb("wo_lo", [P, KT, HID], F32R)
        wsa_hi = sb("wsa_hi", [P, KT, 2 * RANK], F32R)
        wsa_lo = sb("wsa_lo", [P, KT, 2 * RANK], F32R)
        sc_gu = sb("sc_gu", [P, 2 * STEPS, KT], F32)
        sc_d = sb("sc_d", [P, KT, STEPS], F32)
        bias = sb("bias", [P, HID], F32)
        ident = sb("ident", [P, P], F32)
        ident16 = sb("ident16", [P, P], F16)
        identb = sb("identb", [P, P], BF16)
        maskb = sb("maskb", [P, P], BF16)
        const = sb("const", [P, 4, TT], F32)
        CONSTS = (-0.5, LN_EPS, 4.0 / HID, 4.0 * RMS_EPS)
        xn = sb("xn", [P, TT, HID], F32)
        xt_hi = sb("xt_hi", [P, KT, SEQ], F32R)
        xt_lo = sb("xt_lo", [P, KT, SEQ], F32R)
        x16 = sb("x16", [P, 2, 2, KT, SEQ], F16)
        s_hi = sb("s_hi", [RANK, SEQ], F32R)
        s_lo = sb("s_lo", [RANK, SEQ], F32R)
        a_hi = sb("a_hi", [RANK, SEQ], F32R)
        a_lo = sb("a_lo", [RANK, SEQ], F32R)
        v_hi = sb("v_hi", [P, TT, HID], F32R)
        v_lo = sb("v_lo", [P, TT, HID], F32R)
        prob = sb("prob", [P, 2, SEQ], F32)
        pt_hi = sb("pt_hi", [P, SEQ], F32R)
        pt_lo = sb("pt_lo", [P, SEQ], F32R)
        att = sb("att", [P, TT, HID], F32)
        acc = sb("acc", [P, 6, SEQ], F32)
        th = sb("th", [P, SEQ], F32)
        h_hi = sb("h_hi", [P, 3, SEQ], F32R)
        h_lo = sb("h_lo", [P, 3, SEQ], F32R)
        h_bf = sb("h_bf", [P, 3, SEQ], BF16)
        fin = sb("fin", [P, 5, HID], F32)
        stats = sb("stats", [P, TT, 6], F32)
        mv = sb("mv", [P, TT, 2], F32)
        vare = sb("vare", [P, TT], F32)
        rstd = sb("rstd", [P, TT], F32)
        smax = sb("smax", [P, TT], F32)
        nbias = sb("nbias", [P, TT], F32)
        rsum = sb("rsum", [P, TT], F32)
        rinv = sb("rinv", [P, TT], F32)
        ssq = sb("ssq", [P, TT], F32)
        msq = sb("msq", [P, 2, TT], F32)
        r2 = sb("r2", [P, TT], F32)

        y = [pb(f"y{t}", [P, HID], F32) for t in range(TT)]
        ring = [pb(f"ring{n}", [P, SEQ], F32) for n in range(3)]
        aux = pb("aux", [P, SEQ], F32)

        def ring_slot(n):
            return n % 3 if n < NU - 1 else 1

        SLOTS_OF = [ring_slot(n) for n in range(NU)]

        def ring_before(n):
            m = n - 1
            while SLOTS_OF[m % NU] != SLOTS_OF[n]:
                m -= 1
            return m

        fin_w = fin[:, :, :].rearrange("p a b -> p (a b)").bitcast(U32)
        pk_gu = fin_w[:, 0:2 * STEPS * WORDS].rearrange("p (t w) -> p t w", w=WORDS)
        pk_d = fin_w[:, 2 * STEPS * WORDS:2 * STEPS * WORDS + KT * DWORDS].rearrange("p (t w) -> p t w", w=DWORDS)
        x16_1 = x16[:, 1, :, :, :].rearrange("p a b c -> p (a b c)")
        raw_gu = x16_1[0:KT, 0:2 * INNER]
        raw_d = x16_1[0:STEPS, 2 * INNER:2 * INNER + HID]
        w32 = x16_1.bitcast(F32)[:, 0:INNER]
        wsa32 = prob[:, 0, :].rearrange("p (k r) -> p k r", k=KT)
        d32 = prob[0:STEPS, 1, :]
        acc_w = acc[:, :, :].rearrange("p a b -> p (a b)").bitcast(U32)
        HALF = INNER // 2
        code, mag, mag2 = (acc_w[:, n * HALF:(n + 1) * HALF] for n in range(3))
        v16w = att[:, :, :].rearrange("p a b -> p (a b)").bitcast(U32)
        v16 = [v16w[:, n * HALF:(n + 1) * HALF] for n in range(2)]

        d_x0, d_wsa, d_scales, d_gu, d_wo, d_down, d_bo = (
            sem(n) for n in ("d_x0", "d_wsa", "d_scales", "d_gu", "d_wo", "d_down", "d_bo"))
        const_made = sem("const_made")
        set_fill = sem("set_fill")
        set_act = sem("set_act")
        set_dve = sem("set_dve")
        scale_cast = sem("scale_cast")
        wsa_split = sem("wsa_split")
        wsa_done = sem("wsa_done")
        dq = sem("dq")
        v16_ready = sem("v16_ready")
        w32_ready = sem("w32_ready")
        xin_loaded = sem("xin_loaded")
        bn_done, aggr_done, var_done, rstd_done, xn_done = (
            sem(n) for n in ("bn_done", "aggr_done", "var_done", "rstd_done", "xn_done"))
        unit_done, act_evac, dve_evac = sem("unit_done"), sem("act_evac"), sem("dve_evac")
        gsum, usum, m_done, tanh_done, h_done, hbf_done, hhi_done, hlo_done, down_done = (
            sem(n) for n in ("gsum", "usum", "m_done", "tanh_done", "h_done", "hbf_done", "hhi_done", "hlo_done",
                             "down_done"))
        ready = {k: sem(f"{k}_ready") for k in ("SA", "V", "E", "F", "G", "T")}
        sa_hi, sa_lo, vhi_done, vlo_done, max_done, nb_done, exp_done, pthi_done, ptlo_done, rinv_done, att_done = (
            sem(n) for n in ("sa_hi", "sa_lo", "vhi_done", "vlo_done", "max_done", "nb_done", "exp_done", "pthi_done",
                             "ptlo_done", "rinv_done", "att_done"))
        xthi_done, xtlo_done = sem("xthi_done"), sem("xtlo_done")
        sq_done, msq_done, r2_done, ytanh_done, fa_done, fb_done, add_done = (
            sem(n) for n in ("sq_done", "msq_done", "r2_done", "ytanh_done", "fa_done", "fb_done", "add_done"))
        xr_loaded = [sem(f"xr_loaded{n}") for n in range(2)]
        stored = [sem(f"stored{n}") for n in range(2)]

        def wait(eng, s, value):
            if not isinstance(value, int) or value > 0:
                eng.wait_ge(s, value)

        def first_batch():
            return 0, 0, True, False, True

        def in_loop(pair, k):
            return 2 * pair + k, k % 2, True, True, True

        def last_batch():
            return BATCH - 1, (BATCH - 1) % 2, True, True, False

        def drain():
            return BATCH, BATCH % 2, False, True, False

        PAIRS = (BATCH - 2) // 2

        def run_batches(eng, iteration):
            iteration(*first_batch())
            with eng.Fori(0, PAIRS) as pair:
                iteration(*in_loop(pair, 1))
                iteration(*in_loop(pair, 2))
            iteration(*last_batch())
            iteration(*drain())

        def aux_slot(index, more):
            slot = AUX_SLOTS[index]
            return None if slot is None or (slot[0] == "T" and not more) else slot

        def h_slot(i):
            return i % STEPS % 3

        JOB_WO, JOB_GU = 2, 2 + KT
        JOB_D = JOB_GU + STEPS
        D_PARTS = [(0, 4), (4, 8), (8, STEPS)]

        def setup_bank_free(eng, j):
            j -= 4
            if j < 0:
                return
            if j < JOB_GU:
                eng.wait_ge(set_dve, j + 1)
            elif j < JOB_D:
                eng.wait_ge(set_act, KT + j - JOB_GU + 1)
            else:
                eng.wait_ge(set_dve, JOB_GU + j - JOB_D + 1)

        block = ctx.enter_context(nc.Block())

        @block.sync
        def _(sp):
            sp.dma_start(xn[:, :, :], x_v[0]).then_inc(xin_loaded, 16)
            sp.dma_start(raw_gu, gu_scales).then_inc(d_scales, 16)
            sp.dma_start(raw_d, down_scales).then_inc(d_scales, 16)
            sp.dma_start(pk_gu, gu_packed.rearrange("(t p) w -> p t w", p=P)).then_inc(d_gu, 16)
            sp.dma_start(att[:, :, :], Wo.rearrange("(t p) h -> p t h", p=P)).then_inc(d_wo, 16)
            sp.dma_start(wsa32[:, :, 0:RANK], Ws.rearrange("(k p) r -> p k r", p=P)).then_inc(d_wsa, 16)
            sp.dma_start(wsa32[:, :, RANK:2 * RANK], Wa.rearrange("(k p) r -> p k r", p=P)).then_inc(d_wsa, 16)
            sp.dma_start(pk_d, down_packed.rearrange("(t p) w -> p t w", p=P)).then_inc(d_down, 16)
            sp.dma_start(bias[:, :], bo.partition_broadcast(P)).then_inc(d_bo, 16)

            def iteration(b, par, work, prev, more):
                if more:
                    sp.wait_ge(ready["T"], 4 * b + 4)
                    sp.dma_start(xn[:, :, :], x_v[b + 1]).then_inc(xin_loaded, 16)
                if prev:
                    for t in range(TT):
                        wait(sp, add_done, 4 * (b - 1) + max(t - 1, 0))
                        sp.wait_ge(w32_ready, KT)
                        sp.dma_start(fin[:, 2 + t % 2, :], x_v[b - 1][:, t, :])\
                          .then_inc(xr_loaded[t % 2], 16)
                        if t >= 1:
                            sp.wait_ge(add_done, 4 * (b - 1) + t)
                            sp.dma_start(out_v[b - 1][:, t - 1, :], fin[:, (t - 1) % 2, :])\
                              .then_inc(stored[(t - 1) % 2], 16)
                    sp.wait_ge(add_done, 4 * (b - 1) + TT)
                    sp.dma_start(out_v[b - 1][:, TT - 1, :], fin[:, (TT - 1) % 2, :])\
                      .then_inc(stored[(TT - 1) % 2], 16)

            run_batches(sp, iteration)
            for n in range(2):
                sp.wait_ge(stored[n], 16 * TT // 2 * BATCH)

        @block.tensor
        def _(pe):
            pe.wait_ge(const_made, 5)
            pe.wait_ge(d_scales, 32)
            for t in range(2 * STEPS):
                last = nc.tensor.transpose(y[0][:, :].bitcast(F16)[:, t * KT:(t + 1) * KT],
                                           raw_gu[:, t * P:(t + 1) * P], ident16[0:KT, 0:KT])
            last.then_inc(set_fill, 1)
            pe.wait_ge(scale_cast, 1)
            for k in range(KT):
                last = nc.tensor.transpose(y[1][:, k * 16:k * 16 + STEPS], d32[:, k * P:(k + 1) * P],
                                           ident[0:STEPS, 0:STEPS])
            last.then_inc(set_fill, 1)

            def transposes_of_x(B, k):
                pe.wait_ge(xn_done, 4 * B + 4)
                for t in range(TT):
                    last = nc.tensor.transpose(aux[:, t * P:(t + 1) * P], xn[:, t, k * P:(k + 1) * P], ident[:, :])
                last.then_inc(ready["T"], 1)

            for k in range(KT):
                if k:
                    pe.wait_ge(xtlo_done, 2 * k)
                transposes_of_x(0, k)
            pe.wait_ge(d_wo, 16)
            for k in range(KT):
                setup_bank_free(pe, JOB_WO + k)
                for t in range(KT):
                    last = nc.tensor.transpose(y[(JOB_WO + k) % 4][:, t * P:(t + 1) * P],
                                               att[:, t, k * P:(k + 1) * P], ident[:, :])
                last.then_inc(set_fill, 1)
            for i in range(STEPS):
                setup_bank_free(pe, JOB_GU + i)
                pe.wait_ge(v16_ready, i + 1)
                vv = v16[i % 2].bitcast(F16)
                for t in range(2):
                    for k in range(KT):
                        o = (t * KT + k) * P
                        last = nc.tensor.transpose(y[(JOB_GU + i) % 4][:, :].bitcast(F16)[:, o:o + P],
                                                   vv[:, o:o + P], ident16[:, :])
                last.then_inc(set_fill, 1)
            for k in range(KT):
                pe.wait_ge(w32_ready, k + 1)
                for n, (i0, i1) in enumerate(D_PARTS):
                    j = JOB_D + 3 * k + n
                    setup_bank_free(pe, j)
                    for i in range(i0, i1):
                        last = nc.tensor.transpose(y[j % 4][:, (i - i0) * P:(i - i0 + 1) * P],
                                                   w32[:, i * P:(i + 1) * P], ident[:, :])
                    last.then_inc(set_fill, 1)

            def iteration(b, par, work, prev, more):
                def unit(i, u):
                    n, k = UNITS * i + u, u % KT
                    m = ring_before(n)
                    wait(pe, act_evac if m % 2 == 0 else dve_evac, NU // 2 * b + (m - m % 2) // 2 + 1)
                    if i == 0 and u < KT:
                        pe.wait_ge(xtlo_done, 8 * b + 2 * u + 2)
                    o = (i if u < KT else STEPS + i) * P
                    for part in range(2):
                        last = nc.tensor.matmul(ring[SLOTS_OF[n]][:, :], w_gu[:, k, o:o + P], x16[:, par, part, k, :],
                                                start=(part == 0), stop=(part == 1))
                    last.then_inc(unit_done, 1)

                def down(i, t):
                    if i < 2 and not prev:
                        return
                    ii = (i - 2) % STEPS
                    hs = h_slot(ii)
                    if t == 0:
                        pe.wait_ge(hlo_done, STEPS * b + i - 1)
                        pe.wait_ge(hbf_done, STEPS * b + i - 1)
                    if ii == 0:
                        wait(pe, fa_done, 4 * (b - 1) + t + 1)
                    tt = slice(t * P, (t + 1) * P)
                    nc.tensor.matmul(y[t][:, :], h_hi[:, hs, tt], wd_hi[:, ii, :], start=(ii == 0), stop=False)
                    nc.tensor.matmul(y[t][:, :], h_lo[:, hs, tt], wd_hi[:, ii, :], start=False, stop=False)
                    nc.tensor.matmul(y[t][:, :], h_bf[:, hs, tt], wd_lo[:, ii, :], start=False,
                                     stop=(ii == STEPS - 1)).then_inc(down_done, 1)

                def aux_bank_free(index):
                    index -= 1
                    while index >= 0 and aux_slot(index, more) is None:
                        index -= 1
                    kind, n = AUX_SLOTS[index] if index >= 0 else ("T", 3)
                    if kind == "T":
                        pe.wait_ge(xtlo_done, 8 * b + 2 * n + 2 + (8 if index >= 0 else 0))
                    elif kind == "SA":
                        pe.wait_ge(sa_lo, 2 * b + 2)
                    else:
                        pe.wait_ge({"V": vlo_done, "E": exp_done, "F": ptlo_done, "G": att_done}[kind], 4 * b + n + 1)

                def aux_work(index):
                    slot = aux_slot(index, more)
                    if slot is None:
                        yield
                        yield
                        return
                    kind, n = slot
                    aux_bank_free(index)
                    if kind in ("SA", "V"):
                        products = []
                        for k in range(KT):
                            if kind == "SA":
                                pairs = ((wsa_hi, xt_hi), (wsa_hi, xt_lo), (wsa_lo, xt_hi))
                                products += [(w[:, k, :], v[:, k, :]) for w, v in pairs]
                            else:
                                tt = slice(n * P, (n + 1) * P)
                                pairs = ((xt_hi, wo_hi), (xt_lo, wo_hi), (xt_hi, wo_lo))
                                products += [(v[:, k, tt], w[:, k, :]) for v, w in pairs]
                        half = len(products) // 2
                        for m, (lhs, rhs) in enumerate(products):
                            if m == half:
                                yield
                            last = nc.tensor.matmul(aux[:, :], lhs, rhs, start=(m == 0), stop=(m == len(products) - 1))
                    elif kind == "E":
                        if n == 0:
                            pe.wait_ge(sa_lo, 2 * b + 2)
                        cols = max(2 * P, (n + 1) * P)
                        q = slice(n * P, (n + 1) * P)
                        for m, (s, a) in enumerate(((s_hi, a_hi), (s_hi, a_lo), (s_lo, a_hi))):
                            nc.tensor.matmul(aux[:, 0:cols], s[:, q], a[:, 0:cols], start=(m == 0), stop=False)
                        yield
                        last = nc.tensor.matmul(aux[:, q], identb[:, :], maskb[:, :], start=False, stop=True)
                    elif kind == "F":
                        pe.wait_ge(exp_done, 4 * b + n + 1)
                        yield
                        for j in range(n + 1):
                            last = nc.tensor.transpose(aux[:, j * P:(j + 1) * P], prob[:, n % 2, j * P:(j + 1) * P],
                                                       ident[:, :])
                    elif kind == "G":
                        pe.wait_ge(ptlo_done, 4 * b + n + 1)
                        if n == 0 or n == 3:
                            pe.wait_ge(vlo_done, 4 * b + n + 1)
                        products = []
                        for j in range(n + 1):
                            jj = slice(j * P, (j + 1) * P)
                            products += [(pt_hi[:, jj], v_hi[:, j, :]), (pt_lo[:, jj], v_hi[:, j, :]),
                                         (pt_hi[:, jj], v_lo[:, j, :])]
                        half = len(products) // 2
                        for m, (lhs, rhs) in enumerate(products):
                            if m == half:
                                yield
                            last = nc.tensor.matmul(aux[:, :], lhs, rhs, start=(m == 0), stop=(m == len(products) - 1))
                    else:
                        yield
                        pe.wait_ge(xn_done, 4 * (b + 1) + 4)
                        for t in range(TT):
                            last = nc.tensor.transpose(aux[:, t * P:(t + 1) * P], xn[:, t, n * P:(n + 1) * P],
                                                       ident[:, :])
                    last.then_inc(ready[kind], 1)
                    yield

                if not work:
                    for i in range(2):
                        for t in range(TT):
                            down(i, t)
                    return
                for i in range(STEPS):
                    first, second = aux_work(2 * i), aux_work(2 * i + 1)
                    unit(i, 0)
                    next(first)
                    unit(i, 1)
                    next(first)
                    unit(i, 2)
                    down(i, 0)
                    unit(i, 3)
                    down(i, 1)
                    unit(i, 4)
                    next(second)
                    unit(i, 5)
                    next(second)
                    unit(i, 6)
                    down(i, 2)
                    unit(i, 7)
                    down(i, 3)

            pe.wait_ge(set_act, KT + STEPS + 3 * KT)
            pe.wait_ge(set_dve, JOB_GU + 3 * KT)
            pe.wait_ge(wsa_done, 1)
            run_batches(pe, iteration)

        @block.scalar
        def _(act):
            act.wait_ge(d_wsa, 32)
            nc.scalar.activation(wsa_hi[:, :, :], wsa32, ACT.Copy).then_inc(wsa_split, 1)

            def xt_high(B, par, k):
                act.wait_ge(ready["T"], 4 * B + k + 1)
                if k == 0:
                    wait(act, ready["V"], 4 * B)
                nc.scalar.activation(xt_hi[:, k, :], aux[:, :], ACT.Copy).then_inc(xthi_done, 1)
                nc.scalar.activation(x16[:, par, 0, k, :], aux[:, :], ACT.Copy, scale=XSCALE).then_inc(xthi_done, 1)

            for k in range(KT):
                xt_high(0, 0, k)
            for k in range(KT):
                act.wait_ge(set_fill, JOB_WO + k + 1)
                nc.scalar.activation(wo_hi[:, k, :], y[(JOB_WO + k) % 4][:, :], ACT.Copy).then_inc(set_act, 1)
            for i in range(STEPS):
                act.wait_ge(set_fill, JOB_GU + i + 1)
                dst = w_gu[:, :, :].rearrange("p k (t n) -> p t k n", t=2)[:, :, :, i * P:(i + 1) * P]
                src = y[(JOB_GU + i) % 4][:, :].bitcast(F16).rearrange("p (t k n) -> p t k n", t=2, k=KT)
                nc.scalar.activation(dst, src, ACT.Copy).then_inc(set_act, 1)
            for k in range(KT):
                for n, (i0, i1) in enumerate(D_PARTS):
                    j = JOB_D + 3 * k + n
                    act.wait_ge(set_fill, j + 1)
                    src = y[j % 4][:, 0:(i1 - i0) * P].rearrange("p (t n) -> p t n", n=P)
                    nc.scalar.activation(wd_hi[:, i0:i1, k * P:(k + 1) * P], src, ACT.Copy).then_inc(set_act, 1)

            def iteration(b, par, work, prev, more):
                def evac(i, u):
                    sp = (par + i) % 2
                    G = STEPS * b + i
                    if u == 0:
                        wait(act, m_done, G - 1)
                    elif u == 2:
                        wait(act, gsum, G)
                    elif u == 4:
                        wait(act, hlo_done, G - 1)
                        wait(act, hbf_done, G - 1)
                    else:
                        wait(act, usum, G)
                    act.wait_ge(unit_done, NU * b + UNITS * i + u + 1)
                    dst = acc[:, {0: sp, 2: 4, 4: 2 + sp, 6: 5}[u], :]
                    t = i if u < KT else STEPS + i
                    nc.scalar.activation(dst, ring[SLOTS_OF[UNITS * i + u]][:, :], ACT.Copy,
                                         scale=sc_gu[:, t, u % KT:u % KT + 1]).then_inc(act_evac, 1)

                def gate_tanh(i):
                    act.wait_ge(gsum, STEPS * b + i + 1)
                    wait(act, h_done, STEPS * b + i)
                    nc.scalar.activation(th[:, :], acc[:, (par + i) % 2, :], ACT.Tanh, scale=0.5)\
                        .then_inc(tanh_done, 1)

                def hidden_high(i):
                    act.wait_ge(h_done, STEPS * b + i)
                    wait(act, down_done, 44 * b + 4 * i - 8)
                    nc.scalar.activation(h_hi[:, h_slot(i - 1), :], acc[:, 2 + (par + i - 1) % 2, :], ACT.Copy)\
                        .then_inc(hhi_done, 1)

                def aux_read(index):
                    slot = aux_slot(index, more)
                    if slot is None:
                        return
                    kind, n = slot
                    if kind == "T":
                        xt_high(b + 1, 1 - par, n)
                        return
                    if kind == "SA":
                        act.wait_ge(ready[kind], b + 1)
                        wait(act, ready["E"], 4 * b)
                        nc.scalar.activation(s_hi[:, :], aux[0:RANK, :], ACT.Copy).then_inc(sa_hi, 1)
                        nc.scalar.activation(a_hi[:, :], aux[RANK:2 * RANK, :], ACT.Copy).then_inc(sa_hi, 1)
                    elif kind == "V":
                        act.wait_ge(ready[kind], 4 * b + n + 1)
                        wait(act, ready["G"], 4 * b)
                        nc.scalar.activation(v_hi[:, n, :], aux[:, :], ACT.Copy).then_inc(vhi_done, 1)
                    elif kind == "E":
                        act.wait_ge(nb_done, 4 * b + n + 1)
                        wait(act, ready["F"], 4 * b + n - 1)
                        wait(act, rinv_done, 4 * b + n - 3)
                        cols = (n + 1) * P
                        nc.scalar.activation(prob[:, n % 2, 0:cols], aux[:, 0:cols], ACT.Exp,
                                             bias=nbias[:, n:n + 1], scale=QSCALE,
                                             accum_out=rsum[:, n:n + 1]).then_inc(exp_done, 1)
                    elif kind == "F":
                        act.wait_ge(ready[kind], 4 * b + n + 1)
                        wait(act, ready["G"], 4 * b + n)
                        cols = (n + 1) * P
                        nc.scalar.activation(pt_hi[:, 0:cols], aux[:, 0:cols], ACT.Copy).then_inc(pthi_done, 1)

                def sum_of_squares(t):
                    act.wait_ge(down_done, 44 * b + t - 3)
                    wait(act, fb_done, 4 * (b - 1) + t)
                    nc.scalar.activation(fin[:, 4, :], y[t][:, :], ACT.Square, accum_out=ssq[:, t:t + 1])\
                        .then_inc(sq_done, 1)

                def silu_tanh(t):
                    act.wait_ge(r2_done, 4 * (b - 1) + t + 1)
                    wait(act, fb_done, 4 * (b - 1) + t)
                    act.wait_ge(sq_done, 4 * (b - 1) + t + 1)
                    nc.scalar.activation(fin[:, 4, :], y[t][:, :], ACT.Tanh, scale=r2[:, t:t + 1])\
                        .then_inc(ytanh_done, 1)

                if not work:
                    hidden_high(0)
                    for t in range(TT):
                        sum_of_squares(t)
                        silu_tanh(t)
                    return
                for i in range(STEPS):
                    if prev and i == 2:
                        sum_of_squares(0)
                        silu_tanh(0)
                    evac(i, 0)
                    if prev and i == 2:
                        sum_of_squares(1)
                        silu_tanh(1)
                    aux_read(2 * i)
                    evac(i, 2)
                    if prev and i == 2:
                        sum_of_squares(2)
                        silu_tanh(2)
                    evac(i, 4)
                    if i or prev:
                        hidden_high(i)
                    aux_read(2 * i + 1)
                    gate_tanh(i)
                    if prev and i == 2:
                        sum_of_squares(3)
                        silu_tanh(3)
                    evac(i, 6)

            run_batches(act, iteration)

        @block.vector
        def _(dve):
            def bn(B, t):
                dve.wait_ge(xin_loaded, 16 * (B + 1))
                wait(dve, aggr_done, 4 * B)
                nc.vector.bn_stats(stats[:, t, :], xn[:, t, :]).then_inc(bn_done, 1)

            def stats_complete(B):
                dve.wait_ge(bn_done, 4 * B + 4)
                wait(dve, xn_done, 4 * B)
                wait(dve, var_done, B)

            def aggregate(B):
                for t in range(TT):
                    nc.vector.bn_aggr(mv[:, t, :], stats[:, t, :]).then_inc(aggr_done, 1)

            def norm(B, t):
                if t == 0:
                    dve.wait_ge(rstd_done, B + 1)
                    dve.wait_ge(aggr_done, 4 * B + 4)
                nc.vector.tensor_scalar(xn[:, t, :], xn[:, t, :], mv[:, t, 0:1], rstd[:, t:t + 1], ALU.subtract,
                                        ALU.mult).then_inc(xn_done, 1)

            def xt_low(B, par, k):
                dve.wait_ge(xthi_done, 8 * B + 2 * k + 2)
                nc.vector.tensor_tensor(xt_lo[:, k, :], aux[:, :], xt_hi[:, k, :].bitcast(F32), ALU.subtract)\
                    .then_inc(xtlo_done, 1)
                nc.vector.scalar_tensor_tensor(x16[:, par, 1, k, :], aux[:, :], XSCALE, x16[:, par, 0, k, :],
                                               ALU.mult, ALU.subtract).then_inc(xtlo_done, 1)

            for t in range(TT):
                bn(0, t)
            stats_complete(0)
            aggregate(0)
            dve.wait_ge(d_scales, 32)
            dve.wait_ge(d_wsa, 32)
            nc.vector.tensor_copy(d32, raw_d).then_inc(scale_cast, 1)
            for t in range(TT):
                norm(0, t)
            dve.wait_ge(set_fill, 1)
            raw = y[0][:, :].bitcast(F16)[:, 0:2 * STEPS * KT].rearrange("p (t k) -> p t k", k=KT)
            nc.vector.tensor_scalar(sc_gu[:, 0:STEPS, :], raw[:, 0:STEPS, :], 1.0 / XSCALE, None, ALU.mult)
            nc.vector.tensor_scalar(sc_gu[:, STEPS:2 * STEPS, :], raw[:, STEPS:2 * STEPS, :], 0.5 / XSCALE, None,
                                    ALU.mult).then_inc(set_dve, 1)
            dve.wait_ge(set_fill, 2)
            nc.vector.tensor_copy(sc_d[:, :, :],
                                  y[1][:, 0:KT * 16].rearrange("p (k g) -> p k g", g=16)[:, :, 0:STEPS])\
                .then_inc(set_dve, 1)
            for k in range(KT):
                xt_low(0, 0, k)
            dve.wait_ge(wsa_split, 1)
            nc.vector.tensor_tensor(wsa_lo[:, :, :], wsa32, wsa_hi[:, :, :].bitcast(F32), ALU.subtract)\
                .then_inc(wsa_done, 1)
            for k in range(KT):
                dve.wait_ge(set_act, k + 1)
                nc.vector.tensor_tensor(wo_lo[:, k, :], y[(JOB_WO + k) % 4][:, :], wo_hi[:, k, :].bitcast(F32),
                                        ALU.subtract).then_inc(set_dve, 1)

            links = [0]

            def link(instruction):
                links[0] += 1
                instruction.then_inc(dq, 1)
                dve.wait_ge(dq, links[0])

            def dequantise(packed, words, chunk):
                c = code[:, 0:4 * words].rearrange("p (w k) -> p w k", k=4)
                for k in range(4):
                    part = c[:, :, k]
                    if len(packed.shape) == 3:
                        part = part.rearrange("p (t w) -> p t w", t=packed.shape[1])
                    done = nc.vector.tensor_scalar(part, packed, 4 * k, 0x000F000F, ALU.logical_shift_right,
                                                   ALU.bitwise_and)
                link(done)
                cc, m, m2 = (r[:, 0:4 * words] for r in (code, mag, mag2))
                link(nc.vector.tensor_scalar(m, cc, 0x00070007, None, ALU.bitwise_and))
                m16, m216 = m.bitcast(U16), m2.bitcast(U16)
                link(nc.vector.tensor_scalar(m216, m16, float(0x200), float(0x3800), ALU.mult, ALU.add))
                link(nc.vector.tensor_scalar(m16, m16, float(0x3800), float(0x7000), ALU.mult, ALU.min))
                link(nc.vector.tensor_tensor(m16, m16, m216, ALU.min))
                link(nc.vector.tensor_scalar(cc, cc, 0x00080008, 12, ALU.bitwise_and, ALU.logical_shift_left))
                dst = v16[chunk % 2][:, 0:4 * words].bitcast(U16).rearrange("p (w h k) -> p w k h", h=2, k=4)
                pair = [r.bitcast(U16).rearrange("p (w k h) -> p w k h", k=4, h=2) for r in (cc, m)]
                return nc.vector.tensor_tensor(dst, pair[0], pair[1], ALU.bitwise_or)

            dve.wait_ge(d_gu, 16)
            dve.wait_ge(set_fill, JOB_GU)
            for i in range(STEPS):
                if i >= 1:
                    dve.wait_ge(v16_ready, i)
                if i >= 2:
                    dve.wait_ge(set_fill, JOB_GU + i - 1)
                dequantise(pk_gu.rearrange("p (t s) w -> p t s w", t=2)[:, :, i, :], 2 * WORDS, i)\
                    .then_inc(v16_ready, 1)
            dve.wait_ge(d_down, 16)
            dve.wait_ge(v16_ready, STEPS)

            def down_low(k):
                for n, (i0, i1) in enumerate(D_PARTS):
                    dve.wait_ge(set_act, KT + STEPS + 3 * k + n + 1)
                    src = y[(JOB_D + 3 * k + n) % 4][:, 0:(i1 - i0) * P].rearrange("p (t n) -> p t n", n=P)
                    nc.vector.tensor_tensor(wd_lo[:, i0:i1, k * P:(k + 1) * P], src,
                                            wd_hi[:, i0:i1, k * P:(k + 1) * P].bitcast(F32), ALU.subtract)\
                        .then_inc(set_dve, 1)

            for k in range(KT):
                chunk = STEPS + k
                dve.wait_ge(set_fill, min(JOB_GU + chunk - 1, JOB_D))
                link(dequantise(pk_d[:, k, :], DWORDS, chunk))
                if k:
                    dve.wait_ge(set_fill, JOB_D + 3 * k)
                values = v16[chunk % 2][:, 0:4 * DWORDS].bitcast(F16).rearrange("p (g n) -> p g n", n=P)
                nc.vector.tensor_tensor(w32.rearrange("p (g n) -> p g n", n=P), values,
                                        sc_d[:, k, :].unsqueeze(2).broadcast_to([P, STEPS, P]), ALU.mult)\
                    .then_inc(w32_ready, 1)
                if k:
                    down_low(k - 1)
            down_low(KT - 1)

            def iteration(b, par, work, prev, more):
                def evac(i, u):
                    sp = (par + i) % 2
                    dve.wait_ge(act_evac, NU // 2 * b + KT * i + u // 2 + 1)
                    dve.wait_ge(unit_done, NU * b + UNITS * i + u + 1)
                    dst = acc[:, {1: sp, 3: 4, 5: 2 + sp, 7: 5}[u], :]
                    t = i if u < KT else STEPS + i
                    nc.vector.scalar_tensor_tensor(dst, ring[SLOTS_OF[UNITS * i + u]][:, :],
                                                   sc_gu[:, t, u % KT:u % KT + 1], dst, ALU.mult, ALU.add)\
                        .then_inc(dve_evac, 1)

                def hidden(i):
                    dst = acc[:, 2 + (par + i - 1) % 2, :]
                    dve.wait_ge(m_done, STEPS * b + i)
                    dve.wait_ge(tanh_done, STEPS * b + i)
                    nc.vector.scalar_tensor_tensor(dst, th[:, :], 1.0, dst, ALU.add, ALU.mult).then_inc(h_done, 1)
                    dve.wait_ge(h_done, STEPS * b + i)
                    wait(dve, down_done, 44 * b + 4 * i - 8)
                    nc.vector.tensor_copy(h_bf[:, h_slot(i - 1), :], dst).then_inc(hbf_done, 1)

                def aux_read(index):
                    slot = aux_slot(index, more)
                    if slot is None:
                        return
                    kind, n = slot
                    if kind == "T":
                        xt_low(b + 1, 1 - par, n)
                    elif kind == "SA":
                        dve.wait_ge(sa_hi, 2 * b + 2)
                        for (hi, lo), rows in (((s_hi, s_lo), slice(0, RANK)), ((a_hi, a_lo), slice(RANK, 2 * RANK))):
                            nc.vector.tensor_tensor(lo[:, :], aux[rows, :], hi[:, :].bitcast(F32), ALU.subtract)\
                                .then_inc(sa_lo, 1)
                    elif kind == "V":
                        dve.wait_ge(vhi_done, 4 * b + n + 1)
                        nc.vector.tensor_tensor(v_lo[:, n, :], aux[:, :], v_hi[:, n, :].bitcast(F32), ALU.subtract)\
                            .then_inc(vlo_done, 1)
                    elif kind == "E":
                        dve.wait_ge(ready[kind], 4 * b + n + 1)
                        nc.vector.reduce_max(smax[:, n:n + 1], aux[:, 0:(n + 1) * P], AX.X).then_inc(max_done, 1)
                        dve.wait_ge(max_done, 4 * b + n + 1)
                        nc.vector.tensor_scalar(nbias[:, n:n + 1], smax[:, n:n + 1], -QSCALE, None, ALU.mult)\
                            .then_inc(nb_done, 1)
                    elif kind == "F":
                        dve.wait_ge(pthi_done, 4 * b + n + 1)
                        cols = (n + 1) * P
                        nc.vector.tensor_tensor(pt_lo[:, 0:cols], aux[:, 0:cols], pt_hi[:, 0:cols].bitcast(F32),
                                                ALU.subtract).then_inc(ptlo_done, 1)
                    else:
                        dve.wait_ge(exp_done, 4 * b + n + 1)
                        nc.vector.reciprocal(rinv[:, n:n + 1], rsum[:, n:n + 1]).then_inc(rinv_done, 1)
                        dve.wait_ge(rinv_done, 4 * b + n + 1)
                        dve.wait_ge(ready[kind], 4 * b + n + 1)
                        if n == 0:
                            wait(dve, fa_done, 4 * b)
                        nc.vector.scalar_tensor_tensor(att[:, n, :], aux[:, :], rinv[:, n:n + 1], bias[:, :],
                                                       ALU.mult, ALU.add).then_inc(att_done, 1)

                def gated(t):
                    k = 4 * (b - 1) + t
                    dst = fin[:, t % 2, :]
                    dve.wait_ge(ytanh_done, k + 1)
                    wait(dve, stored[t % 2], 16 * (2 * (b - 1) + t // 2))
                    nc.vector.scalar_tensor_tensor(dst, y[t][:, :], r2[:, t:t + 1], att[:, t, :], ALU.mult,
                                                   ALU.mult).then_inc(fa_done, 1)
                    dve.wait_ge(fa_done, k + 1)
                    nc.vector.scalar_tensor_tensor(dst, fin[:, 4, :], 1.0, dst, ALU.add, ALU.mult)\
                        .then_inc(fb_done, 1)

                if not work:
                    hidden(0)
                    for t in range(TT):
                        gated(t)
                    return
                for i in range(STEPS):
                    if prev and i == 2:
                        gated(0)
                    evac(i, 1)
                    if prev and i == 2:
                        gated(1)
                    aux_read(2 * i)
                    evac(i, 3)
                    if more and i == 7:
                        norm(b + 1, 2)
                        norm(b + 1, 3)
                    if prev and i == 2:
                        gated(2)
                    if i or prev:
                        hidden(i)
                    evac(i, 5)
                    aux_read(2 * i + 1)
                    if prev and i == 2:
                        gated(3)
                    if more and i == 5:
                        stats_complete(b + 1)
                    evac(i, 7)
                    if more:
                        if i in (3, 4):
                            bn(b + 1, 2 * (i - 3))
                            bn(b + 1, 2 * (i - 3) + 1)
                        if i == 5:
                            aggregate(b + 1)
                        if i == 6:
                            norm(b + 1, 0)
                            norm(b + 1, 1)

            dve.wait_ge(d_bo, 16)
            run_batches(dve, iteration)

        @block.gpsimd
        def _(pool):
            nc.gpsimd.memset(ident[:, :], 0.0)
            nc.gpsimd.memset(ident16[:, :], 0.0)
            nc.gpsimd.memset(identb[:, :], 0.0)
            nc.gpsimd.memset(maskb[:, :], 0.0)
            for n, value in enumerate(CONSTS):
                last = nc.gpsimd.memset(const[:, n, :], value)
            last.then_inc(const_made, 1)
            pool.wait_ge(const_made, 1)
            for m in (ident, ident16, identb):
                nc.gpsimd.affine_select(out=m[:, :], in_=m[:, :], compare_op=ALU.not_equal, fill=1.0, base=0,
                                        pattern=[[-1, P]], channel_multiplier=1).then_inc(const_made, 1)
            nc.gpsimd.affine_select(out=maskb[:, :], in_=maskb[:, :], compare_op=ALU.is_ge, fill=NEG, base=0,
                                    pattern=[[-1, P]], channel_multiplier=1).then_inc(const_made, 1)

            def rstd_of(B):
                pool.wait_ge(aggr_done, 4 * B + 4)
                wait(pool, xn_done, 4 * B)
                nc.gpsimd.tensor_tensor(vare[:, :], mv[:, :, 1], const[:, 1, :], ALU.add)\
                    .then_inc(var_done, 1)
                pool.wait_ge(var_done, B + 1)
                nc.gpsimd.tensor_tensor(rstd[:, :], vare[:, :], const[:, 0, :], ALU.pow).then_inc(rstd_done, 1)

            rstd_of(0)

            def iteration(b, par, work, prev, more):
                def gate_sum(i):
                    pool.wait_ge(dve_evac, NU // 2 * b + KT * i + 2)
                    dst = acc[:, (par + i) % 2, :]
                    nc.gpsimd.tensor_tensor(dst, dst, acc[:, 4, :], ALU.add).then_inc(gsum, 1)

                def up_sum_and_product(i):
                    G = STEPS * b + i
                    sp = (par + i - 1) % 2
                    dst = acc[:, 2 + sp, :]
                    pool.wait_ge(dve_evac, NU // 2 * b + KT * i)
                    nc.gpsimd.tensor_tensor(dst, dst, acc[:, 5, :], ALU.add).then_inc(usum, 1)
                    pool.wait_ge(usum, G)
                    nc.gpsimd.tensor_tensor(dst, dst, acc[:, sp, :], ALU.mult).then_inc(m_done, 1)

                def hidden_low(i):
                    pool.wait_ge(hhi_done, STEPS * b + i)
                    s = h_slot(i - 1)
                    nc.gpsimd.tensor_tensor(h_lo[:, s, :], acc[:, 2 + (par + i - 1) % 2, :],
                                            h_hi[:, s, :].bitcast(F32), ALU.subtract).then_inc(hlo_done, 1)

                def rms(t):
                    k = 4 * (b - 1) + t
                    pool.wait_ge(sq_done, k + 1)
                    nc.gpsimd.tensor_tensor(msq[:, 0, t:t + 1], ssq[:, t:t + 1], const[:, 2, 0:1], ALU.mult)\
                        .then_inc(msq_done, 1)
                    pool.wait_ge(msq_done, 2 * k + 1)
                    nc.gpsimd.tensor_tensor(msq[:, 1, t:t + 1], msq[:, 0, t:t + 1], const[:, 3, 0:1], ALU.add)\
                        .then_inc(msq_done, 1)
                    pool.wait_ge(msq_done, 2 * k + 2)
                    nc.gpsimd.tensor_tensor(r2[:, t:t + 1], msq[:, 1, t:t + 1], const[:, 0, 0:1], ALU.pow)\
                        .then_inc(r2_done, 1)

                def add_x(t):
                    k = 4 * (b - 1) + t
                    pool.wait_ge(fb_done, k + 1)
                    pool.wait_ge(xr_loaded[t % 2], 16 * (2 * (b - 1) + t // 2 + 1))
                    dst = fin[:, t % 2, :]
                    nc.gpsimd.tensor_tensor(dst, dst, fin[:, 2 + t % 2, :], ALU.add).then_inc(add_done, 1)

                if not work:
                    up_sum_and_product(0)
                    hidden_low(0)
                    for t in range(TT):
                        rms(t)
                        add_x(t)
                    return
                for i in range(STEPS):
                    if prev and i == 2:
                        rms(0)
                    if i or prev:
                        up_sum_and_product(i)
                    if prev and i == 2:
                        rms(1)
                        add_x(0)
                        rms(2)
                        add_x(1)
                    gate_sum(i)
                    if prev and i == 2:
                        rms(3)
                    if i or prev:
                        hidden_low(i)
                    if prev and i == 2:
                        add_x(2)
                        add_x(3)
                    if more and i == 6:
                        rstd_of(b + 1)

            run_batches(pool, iteration)


_INS = ['L0_attn_x', 'L0_attn_Ws', 'L0_attn_Wa', 'L0_attn_Wo', 'L0_attn_bo', 'L0_ffn_gate_up_packed',
        'L0_ffn_gate_up_scales', 'L0_ffn_down_packed', 'L0_ffn_down_scales']


def kernel(**inputs):
    import numpy as _np
    import concourse.bacc as _bacc
    from concourse import mybir as _mybir
    from concourse.bass_utils import run_bass_kernel_spmd as _run

    nc = _bacc.Bacc("TRN2", target_bir_lowering=False, num_devices=1)
    arrays, args = {}, []
    for name in _INS:
        a = _np.ascontiguousarray(inputs[name])
        arrays[f"in_{name}_dram"] = a
        args.append(nc.dram_tensor(f"in_{name}_dram", a.shape, _mybir.dt.from_np(a.dtype), kind="ExternalInput").ap())
    shape = arrays["in_L0_attn_x_dram"].shape
    out = nc.dram_tensor("out_0_dram", shape, _mybir.dt.from_np(_np.dtype("float32")), kind="ExternalOutput").ap()
    gated_attention_ffn(nc, *args, out)
    r = _run(nc, [arrays], core_ids=[0])
    return r.results[0]["out_0_dram"]
```

```python
from contextlib import ExitStack

import concourse.bass as bass
from concourse import mybir

F32 = mybir.dt.float32
F32R = mybir.dt.float32r
F16 = mybir.dt.float16
BF16 = mybir.dt.bfloat16
U16 = mybir.dt.uint16
U32 = mybir.dt.int32
ALU = mybir.AluOpType
ACT = mybir.ActivationFunctionType
AX = mybir.AxisListType

AUX_SLOTS = [("SA", 0), ("V", 0), ("V", 1), ("E", 0), ("V", 2), ("E", 1), ("F", 0), ("V", 3), ("G", 0), ("F", 1),
             ("E", 2), ("G", 1), ("F", 2), ("E", 3), ("G", 2), ("T", 0), ("F", 3), ("T", 1), ("G", 3), ("T", 2),
             ("T", 3), None]


def gated_attention_ffn(nc, x, Ws, Wa, Wo, bo, gu_packed, gu_scales, down_packed, down_scales, out):
    BATCH, SEQ, HID = x.shape
    RANK = Ws.shape[1]
    INNER = gu_packed.shape[0] // 2
    P = 128
    TT = SEQ // P
    KT = HID // P
    STEPS = INNER // P
    UNITS = 2 * KT
    NU = UNITS * STEPS
    QSCALE = float(RANK) ** -0.5
    XSCALE = 1024.0
    LN_EPS, RMS_EPS = 1e-5, 1e-6
    NEG = -3.0e38
    WORDS = HID // 8
    DWORDS = INNER // 8

    x_v = x.rearrange("b (t p) h -> b p t h", p=P)
    out_v = out.rearrange("b (t p) h -> b p t h", p=P)

    ctx = ExitStack()
    with ctx:
        def sb(name, shape, dt):
            return ctx.enter_context(nc.sbuf_tensor(name, shape, dt))

        def pb(name, shape, dt):
            return ctx.enter_context(nc.psum_tensor(name, shape, dt))

        def sem(name):
            return ctx.enter_context(nc.semaphore(name))

        w_gu = sb("w_gu", [P, KT, 2 * INNER], F16)
        wd_hi = sb("wd_hi", [P, STEPS, HID], F32R)
        wd_lo = sb("wd_lo", [P, STEPS, HID], BF16)
        wo_hi = sb("wo_hi", [P, KT, HID], F32R)
        wo_lo = sb("wo_lo", [P, KT, HID], F32R)
        wsa_hi = sb("wsa_hi", [P, KT, 2 * RANK], F32R)
        wsa_lo = sb("wsa_lo", [P, KT, 2 * RANK], F32R)
        sc_gu = sb("sc_gu", [P, 2 * STEPS, KT], F32)
        sc_d = sb("sc_d", [P, KT, STEPS], F32)
        bias = sb("bias", [P, HID], F32)
        ident = sb("ident", [P, P], F32)
        ident16 = sb("ident16", [P, P], F16)
        identb = sb("identb", [P, P], BF16)
        maskb = sb("maskb", [P, P], BF16)
        const = sb("const", [P, 4, TT], F32)
        CONSTS = (-0.5, LN_EPS, 4.0 / HID, 4.0 * RMS_EPS)
        xn = sb("xn", [P, TT, HID], F32)
        xt_hi = sb("xt_hi", [P, KT, SEQ], F32R)
        xt_lo = sb("xt_lo", [P, KT, SEQ], F32R)
        x16 = sb("x16", [P, 2, 2, KT, SEQ], F16)
        s_hi = sb("s_hi", [RANK, SEQ], F32R)
        s_lo = sb("s_lo", [RANK, SEQ], F32R)
        a_hi = sb("a_hi", [RANK, SEQ], F32R)
        a_lo = sb("a_lo", [RANK, SEQ], F32R)
        v_hi = sb("v_hi", [P, TT, HID], F32R)
        v_lo = sb("v_lo", [P, TT, HID], F32R)
        prob = sb("prob", [P, 2, SEQ], F32)
        pt_hi = sb("pt_hi", [P, SEQ], F32R)
        pt_lo = sb("pt_lo", [P, SEQ], F32R)
        att = sb("att", [P, TT, HID], F32)
        acc = sb("acc", [P, 6, SEQ], F32)
        th = sb("th", [P, SEQ], F32)
        h_hi = sb("h_hi", [P, 3, SEQ], F32R)
        h_lo = sb("h_lo", [P, 3, SEQ], F32R)
        h_bf = sb("h_bf", [P, 3, SEQ], BF16)
        fin = sb("fin", [P, 7, HID], F32)
        junk = sb("junk", [P, HID], BF16)
        mag = sb("mag", [P, 3 * SEQ // 2], U32)
        stats = sb("stats", [P, TT, 6], F32)
        mv = sb("mv", [P, TT, 2], F32)
        vare = sb("vare", [P, TT], F32)
        rstd = sb("rstd", [P, TT], F32)
        smax = sb("smax", [P, TT], F32)
        nbias = sb("nbias", [P, TT], F32)
        rsum = sb("rsum", [P, TT], F32)
        rinv = sb("rinv", [P, TT], F32)
        ssq = sb("ssq", [P, TT], F32)
        msq = sb("msq", [P, 2, TT], F32)
        r2 = sb("r2", [P, TT], F32)

        y = [pb(f"y{t}", [P, HID], F32) for t in range(TT)]
        ring = [pb(f"ring{n}", [P, SEQ], F32) for n in range(3)]
        aux = pb("aux", [P, SEQ], F32)

        def ring_slot(n):
            return n % 3 if n < NU - 1 else 1

        SLOTS_OF = [ring_slot(n) for n in range(NU)]

        def ring_before(n):
            m = n - 1
            while SLOTS_OF[m % NU] != SLOTS_OF[n]:
                m -= 1
            return m

        fin_w = fin[:, :, :].rearrange("p a b -> p (a b)").bitcast(U32)
        pk_gu = fin_w[:, 0:2 * STEPS * WORDS].rearrange("p (t w) -> p t w", w=WORDS)
        at_d = 2 * STEPS * WORDS
        pk_d = fin_w[:, at_d:at_d + KT * DWORDS].rearrange("p (t w) -> p t w", w=DWORDS)
        at_v = at_d + KT * DWORDS
        CHUNK = (2 * KT + KT) * P
        value16 = fin_w[:, at_v:at_v + CHUNK // 2].bitcast(U16)
        w32 = fin_w[:, at_v + CHUNK // 2:at_v + CHUNK // 2 + HID].bitcast(F32)
        mag16 = mag[:, :].bitcast(U16)
        x16_1 = x16[:, 1, :, :, :].rearrange("p a b c -> p (a b c)")
        raw_gu = x16_1[0:KT, 0:2 * INNER]
        raw_d = x16_1[0:STEPS, 2 * INNER:2 * INNER + HID]
        wsa32 = prob[:, 0, :].rearrange("p (k r) -> p k r", k=KT)
        d32 = prob[0:STEPS, 1, :]

        d_wsa, d_scales, d_gu, d_wo, d_down, d_bo = (
            sem(n) for n in ("d_wsa", "d_scales", "d_gu", "d_wo", "d_down", "d_bo"))
        const_made = sem("const_made")
        scale_cast = sem("scale_cast")
        scale_fill, scale_done = sem("scale_fill"), sem("scale_done")
        wsa_split, wsa_done = sem("wsa_split"), sem("wsa_done")
        wo_fill, wohi_done, wolo_done = sem("wo_fill"), sem("wohi_done"), sem("wolo_done")
        codes, biased, dq = sem("codes"), sem("biased"), sem("dq")
        value_ready, w32_ready = sem("value_ready"), sem("w32_ready")
        gu_fill, gu_done = sem("gu_fill"), sem("gu_done")
        d_fill, dhi_done, dlo_done = sem("d_fill"), sem("dhi_done"), sem("dlo_done")
        xin_loaded = sem("xin_loaded")
        bn_done, aggr_done, var_done, rstd_done, xn_done = (
            sem(n) for n in ("bn_done", "aggr_done", "var_done", "rstd_done", "xn_done"))
        unit_done, act_evac, dve_evac = sem("unit_done"), sem("act_evac"), sem("dve_evac")
        gsum, usum, m_done, tanh_done, h_done, hbf_done, hhi_done, hlo_done, down_done = (
            sem(n) for n in ("gsum", "usum", "m_done", "tanh_done", "h_done", "hbf_done", "hhi_done", "hlo_done",
                             "down_done"))
        ready = {k: sem(f"{k}_ready") for k in ("SA", "V", "E", "F", "G", "T")}
        sa_hi, sa_lo, vhi_done, vlo_done, max_done, nb_done, exp_done, pthi_done, ptlo_done, rinv_done, att_done = (
            sem(n) for n in ("sa_hi", "sa_lo", "vhi_done", "vlo_done", "max_done", "nb_done", "exp_done", "pthi_done",
                             "ptlo_done", "rinv_done", "att_done"))
        xthi_done, xtlo_done = sem("xthi_done"), sem("xtlo_done")
        sq_done, msq_done, r2_done, ytanh_done, fa_done, fb_done, add_done = (
            sem(n) for n in ("sq_done", "msq_done", "r2_done", "ytanh_done", "fa_done", "fb_done", "add_done"))
        xr_loaded = [sem(f"xr_loaded{n}") for n in range(2)]
        stored = [sem(f"stored{n}") for n in range(TT)]
        ycopy_done = sem("ycopy_done")

        def wait(eng, s, value):
            if not isinstance(value, int) or value > 0:
                eng.wait_ge(s, value)

        def first_batch():
            return 0, 0, True, False, True

        def in_loop(pair, k):
            return 2 * pair + k, k % 2, True, True, True

        def last_batch():
            return BATCH - 1, (BATCH - 1) % 2, True, True, False

        def drain():
            return BATCH, BATCH % 2, False, True, False

        PAIRS = (BATCH - 2) // 2

        def run_batches(eng, iteration):
            iteration(*first_batch())
            with eng.Fori(0, PAIRS) as pair:
                iteration(*in_loop(pair, 1))
                iteration(*in_loop(pair, 2))
            iteration(*last_batch())
            iteration(*drain())

        def aux_slot(index, more):
            slot = AUX_SLOTS[index]
            return None if slot is None or (slot[0] == "T" and not more) else slot

        def h_slot(i):
            return i % STEPS % 3

        def is_first(b):
            return isinstance(b, int) and b == 0

        def stored_chunk(b, i):
            return i + 1 if is_first(b) and i + 1 < STEPS else None

        def valued_chunk(b, i):
            return i + 2 if is_first(b) and i + 2 < STEPS else None

        x0_bank = wo_bank = y

        block = ctx.enter_context(nc.Block())

        @block.sync
        def _(sp):
            sp.dma_start(xn[:, :, :], x_v[0]).then_inc(xin_loaded, 16)
            sp.dma_start(raw_gu, gu_scales).then_inc(d_scales, 16)
            sp.dma_start(raw_d, down_scales).then_inc(d_scales, 16)
            sp.dma_start(att[:, :, :], Wo.rearrange("(t p) h -> p t h", p=P)).then_inc(d_wo, 16)
            sp.dma_start(bias[:, :], bo.partition_broadcast(P)).then_inc(d_bo, 16)

            def iteration(b, par, work, prev, more):
                if more:
                    sp.wait_ge(ready["T"], 4 * b + 4)
                    sp.dma_start(xn[:, :, :], x_v[b + 1]).then_inc(xin_loaded, 16)
                if prev:
                    for t in range(TT):
                        wait(sp, add_done, 4 * (b - 1) + max(t - 1, 0))
                        sp.wait_ge(dlo_done, STEPS)
                        sp.dma_start(fin[:, 4 + t % 2, :], x_v[b - 1][:, t, :])\
                          .then_inc(xr_loaded[t % 2], 16)
                        if t >= 1:
                            sp.wait_ge(add_done, 4 * (b - 1) + t)
                            sp.dma_start(out_v[b - 1][:, t - 1, :], fin[:, t - 1, :])\
                              .then_inc(stored[t - 1], 16)
                    sp.wait_ge(add_done, 4 * (b - 1) + TT)
                    sp.dma_start(out_v[b - 1][:, TT - 1, :], fin[:, TT - 1, :])\
                      .then_inc(stored[TT - 1], 16)

            run_batches(sp, iteration)
            for t in range(TT):
                sp.wait_ge(stored[t], 16 * BATCH)

        @block.tensor
        def _(pe):
            pe.wait_ge(const_made, 5)
            pe.wait_ge(xn_done, 4)
            for k in range(KT):
                for t in range(TT):
                    last = nc.tensor.transpose(x0_bank[k][:, t * P:(t + 1) * P], xn[:, t, k * P:(k + 1) * P],
                                               ident[:, :])
                last.then_inc(ready["T"], 1)
            pe.wait_ge(d_scales, 32)
            for t in range(2 * STEPS):
                last = nc.tensor.transpose(ring[0][:, :].bitcast(F16)[:, t * KT:(t + 1) * KT],
                                           raw_gu[:, t * P:(t + 1) * P], ident16[0:KT, 0:KT])
            last.then_inc(scale_fill, 1)
            pe.wait_ge(scale_cast, 1)
            for k in range(KT):
                last = nc.tensor.transpose(ring[1][:, k * 16:k * 16 + STEPS], d32[:, k * P:(k + 1) * P],
                                           ident[0:STEPS, 0:STEPS])
            last.then_inc(scale_fill, 1)
            def transpose_gate_up(c, bank):
                pe.wait_ge(value_ready, c + 1)
                values = value16.bitcast(F16)
                for n in range(2 * KT):
                    last = nc.tensor.transpose(bank[:, :].bitcast(F16)[:, n * P:(n + 1) * P],
                                               values[:, n * P:(n + 1) * P], ident16[:, :])
                last.then_inc(gu_fill, 1)

            def transpose_down(c, bank):
                pe.wait_ge(w32_ready, c + 1)
                for k in range(KT):
                    last = nc.tensor.transpose(bank[:, k * P:(k + 1) * P], w32[:, k * P:(k + 1) * P], ident[:, :])
                last.then_inc(d_fill, 1)

            transpose_gate_up(0, ring[2])
            pe.wait_ge(d_wo, 16)
            for k in range(KT):
                pe.wait_ge(xtlo_done, 2 * k + 2)
                for t in range(KT):
                    last = nc.tensor.transpose(wo_bank[k][:, t * P:(t + 1) * P],
                                               att[:, t, k * P:(k + 1) * P], ident[:, :])
                last.then_inc(wo_fill, 1)
            transpose_down(0, aux)

            def iteration(b, par, work, prev, more):
                def unit(i, u):
                    n, k = UNITS * i + u, u % KT
                    m = ring_before(n)
                    wait(pe, act_evac if m % 2 == 0 else dve_evac, NU // 2 * b + (m - m % 2) // 2 + 1)
                    if i == 0 and u < KT:
                        pe.wait_ge(xtlo_done, 8 * b + 2 * u + 2)
                    if is_first(b) and u == 0:
                        pe.wait_ge(gu_done, i + 1)
                        pe.wait_ge(scale_done, 2)
                    o = (i if u < KT else STEPS + i) * P
                    for part in range(2):
                        last = nc.tensor.matmul(ring[SLOTS_OF[n]][:, :], w_gu[:, k, o:o + P], x16[:, par, part, k, :],
                                                start=(part == 0), stop=(part == 1))
                    last.then_inc(unit_done, 1)

                def down(i, t):
                    if i < 2 and not prev:
                        return
                    ii = (i - 2) % STEPS
                    hs = h_slot(ii)
                    if t == 0:
                        pe.wait_ge(hlo_done, STEPS * b + i - 1)
                        pe.wait_ge(hbf_done, STEPS * b + i - 1)
                    if is_first(b) and t == 0:
                        pe.wait_ge(dlo_done, ii + 1)
                    if ii == 0:
                        wait(pe, ycopy_done, 4 * (b - 1) + t + 1)
                    tt = slice(t * P, (t + 1) * P)
                    nc.tensor.matmul(y[t][:, :], h_hi[:, hs, tt], wd_hi[:, ii, :], start=(ii == 0), stop=False)
                    nc.tensor.matmul(y[t][:, :], h_lo[:, hs, tt], wd_hi[:, ii, :], start=False, stop=False)
                    nc.tensor.matmul(y[t][:, :], h_bf[:, hs, tt], wd_lo[:, ii, :], start=False,
                                     stop=(ii == STEPS - 1)).then_inc(down_done, 1)

                def aux_bank_free(index, after_chunk=True):
                    if after_chunk and index % 2 == 0 and (index == 0 or stored_chunk(b, index // 2) is not None)\
                            and is_first(b):
                        pe.wait_ge(dlo_done, index // 2 + 2)
                        return
                    index -= 1
                    while index >= 0 and aux_slot(index, more) is None:
                        index -= 1
                    kind, n = AUX_SLOTS[index] if index >= 0 else ("T", 3)
                    if kind == "T":
                        pe.wait_ge(xtlo_done, 8 * b + 2 * n + 2 + (8 if index >= 0 else 0))
                    elif kind == "SA":
                        pe.wait_ge(sa_lo, 2 * b + 2)
                    else:
                        pe.wait_ge({"V": vlo_done, "E": exp_done, "F": ptlo_done, "G": att_done}[kind], 4 * b + n + 1)

                def aux_work(index):
                    slot = aux_slot(index, more)
                    if slot is None:
                        yield
                        yield
                        return
                    kind, n = slot
                    aux_bank_free(index)
                    if is_first(b) and kind == "SA":
                        pe.wait_ge(wsa_done, 1)
                    if is_first(b) and kind == "V":
                        pe.wait_ge(wolo_done, KT)
                    if kind in ("SA", "V"):
                        products = []
                        for k in range(KT):
                            if kind == "SA":
                                pairs = ((wsa_hi, xt_hi), (wsa_hi, xt_lo), (wsa_lo, xt_hi))
                                products += [(w[:, k, :], v[:, k, :]) for w, v in pairs]
                            else:
                                tt = slice(n * P, (n + 1) * P)
                                pairs = ((xt_hi, wo_hi), (xt_lo, wo_hi), (xt_hi, wo_lo))
                                products += [(v[:, k, tt], w[:, k, :]) for v, w in pairs]
                        half = len(products) // 2
                        for m, (lhs, rhs) in enumerate(products):
                            if m == half:
                                yield
                            last = nc.tensor.matmul(aux[:, :], lhs, rhs, start=(m == 0), stop=(m == len(products) - 1))
                    elif kind == "E":
                        if n == 0:
                            pe.wait_ge(sa_lo, 2 * b + 2)
                        cols = max(2 * P, (n + 1) * P)
                        q = slice(n * P, (n + 1) * P)
                        for m, (s, a) in enumerate(((s_hi, a_hi), (s_hi, a_lo), (s_lo, a_hi))):
                            nc.tensor.matmul(aux[:, 0:cols], s[:, q], a[:, 0:cols], start=(m == 0), stop=False)
                        nc.tensor.matmul(aux[:, q], identb[:, :], maskb[:, :], start=False, stop=True)\
                            .then_inc(ready[kind], 1)
                        yield
                        yield
                        return
                    elif kind == "F":
                        pe.wait_ge(exp_done, 4 * b + n + 1)
                        for j in range(n + 1):
                            last = nc.tensor.transpose(aux[:, j * P:(j + 1) * P], prob[:, n % 2, j * P:(j + 1) * P],
                                                       ident[:, :])
                        last.then_inc(ready[kind], 1)
                        yield
                        yield
                        return
                    elif kind == "G":
                        pe.wait_ge(ptlo_done, 4 * b + n + 1)
                        if n == 0 or n == 3:
                            pe.wait_ge(vlo_done, 4 * b + n + 1)
                        products = []
                        for j in range(n + 1):
                            jj = slice(j * P, (j + 1) * P)
                            products += [(pt_hi[:, jj], v_hi[:, j, :]), (pt_lo[:, jj], v_hi[:, j, :]),
                                         (pt_hi[:, jj], v_lo[:, j, :])]
                        half = len(products) // 2
                        for m, (lhs, rhs) in enumerate(products):
                            if m == half:
                                yield
                            last = nc.tensor.matmul(aux[:, :], lhs, rhs, start=(m == 0), stop=(m == len(products) - 1))
                    else:
                        pe.wait_ge(xn_done, 4 * (b + 1) + 4)
                        for t in range(TT):
                            last = nc.tensor.transpose(aux[:, t * P:(t + 1) * P], xn[:, t, n * P:(n + 1) * P],
                                                       ident[:, :])
                        last.then_inc(ready[kind], 1)
                        yield
                        yield
                        return
                    last.then_inc(ready[kind], 1)
                    yield

                if not work:
                    for t in range(TT):
                        for i in range(2):
                            down(i, t)
                    return
                for i in range(STEPS):
                    first, second = aux_work(2 * i), aux_work(2 * i + 1)
                    if is_first(b):
                        c = stored_chunk(b, i)
                        unit(i, 0)
                        if c is not None:
                            if i:
                                aux_bank_free(2 * i, False)
                            else:
                                pe.wait_ge(dlo_done, 1)
                            transpose_gate_up(c, aux)
                        unit(i, 1)
                        down(i, 0)
                        if c is not None:
                            pe.wait_ge(gu_done, c + 1)
                            transpose_down(c, aux)
                        unit(i, 2)
                        down(i, 1)
                        next(first)
                        unit(i, 3)
                        next(first)
                        unit(i, 4)
                        down(i, 2)
                        unit(i, 5)
                        next(second)
                        unit(i, 6)
                        next(second)
                        unit(i, 7)
                        down(i, 3)
                        continue
                    unit(i, 0)
                    next(first)
                    unit(i, 1)
                    next(first)
                    unit(i, 2)
                    down(i, 0)
                    unit(i, 3)
                    down(i, 1)
                    unit(i, 4)
                    next(second)
                    unit(i, 5)
                    next(second)
                    unit(i, 6)
                    down(i, 2)
                    unit(i, 7)
                    down(i, 3)

            run_batches(pe, iteration)

        @block.scalar
        def _(act):
            act.dma_start(pk_gu, gu_packed.rearrange("(t p) w -> p t w", p=P)).then_inc(d_gu, 16)
            act.dma_start(pk_d, down_packed.rearrange("(t p) w -> p t w", p=P)).then_inc(d_down, 16)
            act.dma_start(wsa32[:, :, 0:RANK], Ws.rearrange("(k p) r -> p k r", p=P)).then_inc(d_wsa, 16)
            act.dma_start(wsa32[:, :, RANK:2 * RANK], Wa.rearrange("(k p) r -> p k r", p=P)).then_inc(d_wsa, 16)

            def xt_high(B, par, k, bank):
                act.wait_ge(ready["T"], 4 * B + k + 1)
                if k == 0:
                    wait(act, ready["V"], 4 * B)
                nc.scalar.activation(xt_hi[:, k, :], bank[:, :], ACT.Copy).then_inc(xthi_done, 1)
                nc.scalar.activation(x16[:, par, 0, k, :], bank[:, :], ACT.Copy, scale=XSCALE).then_inc(xthi_done, 1)

            def biased_codes(c):
                act.wait_ge(codes, c + 1)
                if c:
                    act.wait_ge(gu_fill, c)
                    act.wait_ge(w32_ready, c)
                nc.scalar.activation(value16, mag16, ACT.Copy, bias=float(0x3800), scale=float(0x200))\
                    .then_inc(biased, 1)

            def store_gate_up(c, bank):
                act.wait_ge(gu_fill, c + 1)
                dst = w_gu[:, :, :].rearrange("p k (t n) -> p t k n", t=2)[:, :, :, c * P:(c + 1) * P]
                src = bank[:, :].bitcast(F16).rearrange("p (t k n) -> p t k n", t=2, k=KT)
                nc.scalar.activation(dst, src, ACT.Copy).then_inc(gu_done, 1)

            def store_down(c, bank):
                act.wait_ge(d_fill, c + 1)
                nc.scalar.activation(wd_hi[:, c, :], bank[:, :], ACT.Copy).then_inc(dhi_done, 1)

            for k in range(2):
                xt_high(0, 0, k, x0_bank[k])
            biased_codes(0)
            for k in range(2, KT):
                xt_high(0, 0, k, x0_bank[k])
            act.wait_ge(d_wsa, 32)
            nc.scalar.activation(wsa_hi[:, :, :], wsa32, ACT.Copy).then_inc(wsa_split, 1)
            store_gate_up(0, ring[2])
            for k in range(KT):
                act.wait_ge(wo_fill, k + 1)
                nc.scalar.activation(wo_hi[:, k, :], wo_bank[k][:, :], ACT.Copy).then_inc(wohi_done, 1)
                if k == 0:
                    biased_codes(1)
            store_down(0, aux)

            def iteration(b, par, work, prev, more):
                def evac(i, u):
                    sp = (par + i) % 2
                    G = STEPS * b + i
                    if u == 0:
                        wait(act, m_done, G - 1)
                    elif u == 2:
                        wait(act, gsum, G)
                    elif u == 4:
                        wait(act, hlo_done, G - 1)
                        wait(act, hbf_done, G - 1)
                    else:
                        wait(act, usum, G)
                    act.wait_ge(unit_done, NU * b + UNITS * i + u + 1)
                    dst = acc[:, {0: sp, 2: 4, 4: 2 + sp, 6: 5}[u], :]
                    t = i if u < KT else STEPS + i
                    nc.scalar.activation(dst, ring[SLOTS_OF[UNITS * i + u]][:, :], ACT.Copy,
                                         scale=sc_gu[:, t, u % KT:u % KT + 1]).then_inc(act_evac, 1)

                def gate_tanh(i):
                    act.wait_ge(gsum, STEPS * b + i + 1)
                    wait(act, h_done, STEPS * b + i)
                    nc.scalar.activation(th[:, :], acc[:, (par + i) % 2, :], ACT.Tanh, scale=0.5)\
                        .then_inc(tanh_done, 1)

                def hidden_high(i):
                    act.wait_ge(h_done, STEPS * b + i)
                    wait(act, down_done, 44 * b + 4 * i - 8)
                    nc.scalar.activation(h_hi[:, h_slot(i - 1), :], acc[:, 2 + (par + i - 1) % 2, :], ACT.Copy)\
                        .then_inc(hhi_done, 1)

                def aux_read(index):
                    slot = aux_slot(index, more)
                    if slot is None:
                        return
                    kind, n = slot
                    if kind == "T":
                        xt_high(b + 1, 1 - par, n, aux)
                        return
                    if kind == "SA":
                        act.wait_ge(ready[kind], b + 1)
                        wait(act, ready["E"], 4 * b)
                        nc.scalar.activation(s_hi[:, :], aux[0:RANK, :], ACT.Copy).then_inc(sa_hi, 1)
                        nc.scalar.activation(a_hi[:, :], aux[RANK:2 * RANK, :], ACT.Copy).then_inc(sa_hi, 1)
                    elif kind == "V":
                        act.wait_ge(ready[kind], 4 * b + n + 1)
                        wait(act, ready["G"], 4 * b)
                        nc.scalar.activation(v_hi[:, n, :], aux[:, :], ACT.Copy).then_inc(vhi_done, 1)
                    elif kind == "E":
                        act.wait_ge(nb_done, 4 * b + n + 1)
                        wait(act, ready["F"], 4 * b + n - 1)
                        wait(act, rinv_done, 4 * b + n - 3)
                        cols = (n + 1) * P
                        nc.scalar.activation(prob[:, n % 2, 0:cols], aux[:, 0:cols], ACT.Exp,
                                             bias=nbias[:, n:n + 1], scale=QSCALE,
                                             accum_out=rsum[:, n:n + 1]).then_inc(exp_done, 1)
                    elif kind == "F":
                        act.wait_ge(ready[kind], 4 * b + n + 1)
                        wait(act, ready["G"], 4 * b + n)
                        cols = (n + 1) * P
                        nc.scalar.activation(pt_hi[:, 0:cols], aux[:, 0:cols], ACT.Copy).then_inc(pthi_done, 1)

                def copy_y(t):
                    act.wait_ge(down_done, 44 * b + t - 3 if work else 44 * b - 8 + 2 * t + 2)
                    wait(act, stored[t], 16 * (b - 1))
                    nc.scalar.activation(fin[:, t, :], y[t][:, :], ACT.Copy).then_inc(ycopy_done, 1)

                def sum_of_squares(t):
                    act.wait_ge(ycopy_done, 4 * (b - 1) + t + 1)
                    wait(act, sq_done, 4 * (b - 1) + t)
                    wait(act, msq_done, 8 * (b - 1))
                    nc.scalar.activation(junk[:, :], fin[:, t, :], ACT.Square, accum_out=ssq[:, t:t + 1])\
                        .then_inc(sq_done, 1)

                def silu_tanh(t):
                    act.wait_ge(r2_done, 4 * (b - 1) + t + 1)
                    wait(act, fb_done, 4 * (b - 1) + t)
                    nc.scalar.activation(fin[:, 6, :], fin[:, t, :], ACT.Tanh, scale=r2[:, t:t + 1])\
                        .then_inc(ytanh_done, 1)

                if not work:
                    hidden_high(0)
                    for t in range(TT + 1):
                        if t < TT:
                            copy_y(t)
                            sum_of_squares(t)
                        if t:
                            silu_tanh(t - 1)
                    return
                for i in range(STEPS):
                    if is_first(b):
                        evac(i, 0)
                        c = stored_chunk(b, i)
                        if c is not None:
                            store_gate_up(c, aux)
                            store_down(c, aux)
                        evac(i, 2)
                        if valued_chunk(b, i) is not None:
                            biased_codes(valued_chunk(b, i))
                        aux_read(2 * i)
                        evac(i, 4)
                        if i:
                            hidden_high(i)
                        gate_tanh(i)
                        evac(i, 6)
                        aux_read(2 * i + 1)
                        continue
                    evac(i, 0)
                    if prev and i == 2:
                        copy_y(2)
                    aux_read(2 * i)
                    evac(i, 2)
                    if prev:
                        if i == 1:
                            copy_y(0)
                        if i == 2:
                            copy_y(3)
                        if i in (3, 4, 5):
                            silu_tanh(i - 3)
                        if i == 7:
                            silu_tanh(3)
                    evac(i, 4)
                    if i or prev:
                        hidden_high(i)
                    aux_read(2 * i + 1)
                    gate_tanh(i)
                    evac(i, 6)
                    if prev:
                        if i == 1:
                            copy_y(1)
                        if i in (2, 3, 4, 5):
                            sum_of_squares(i - 2)

            run_batches(act, iteration)

        @block.vector
        def _(dve):
            def bn(B, t):
                dve.wait_ge(xin_loaded, 16 * (B + 1))
                wait(dve, aggr_done, 4 * B)
                nc.vector.bn_stats(stats[:, t, :], xn[:, t, :]).then_inc(bn_done, 1)

            def stats_complete(B):
                dve.wait_ge(bn_done, 4 * B + 4)
                wait(dve, xn_done, 4 * B)
                wait(dve, var_done, B)

            def aggregate(B):
                for t in range(TT):
                    nc.vector.bn_aggr(mv[:, t, :], stats[:, t, :]).then_inc(aggr_done, 1)

            def norm(B, t):
                if t == 0:
                    dve.wait_ge(rstd_done, B + 1)
                    dve.wait_ge(aggr_done, 4 * B + 4)
                nc.vector.tensor_scalar(xn[:, t, :], xn[:, t, :], mv[:, t, 0:1], rstd[:, t:t + 1], ALU.subtract,
                                        ALU.mult).then_inc(xn_done, 1)

            def xt_low(B, par, k, bank):
                dve.wait_ge(xthi_done, 8 * B + 2 * k + 2)
                nc.vector.tensor_tensor(xt_lo[:, k, :], bank[:, :], xt_hi[:, k, :].bitcast(F32), ALU.subtract)\
                    .then_inc(xtlo_done, 1)
                nc.vector.scalar_tensor_tensor(x16[:, par, 1, k, :], bank[:, :], XSCALE, x16[:, par, 0, k, :],
                                               ALU.mult, ALU.subtract).then_inc(xtlo_done, 1)

            links = [0]

            def link(instruction):
                links[0] += 1
                instruction.then_inc(dq, 1)
                dve.wait_ge(dq, links[0])

            def chunk_parts(c):
                gu = pk_gu.rearrange("p (t s) w -> p t s w", t=2)[:, :, c, :].bitcast(U16)
                down = pk_d[:, :, 16 * c:16 * c + 16].bitcast(U16)
                to_gu = mag16[:, 0:8 * P].rearrange("p (t w k) -> p t w k", t=2, k=4)
                to_down = mag16[:, 8 * P:12 * P].rearrange("p (t w k) -> p t w k", t=KT, k=4)
                return (gu, to_gu), (down, to_down)

            def magnitude_codes(c):
                if c:
                    dve.wait_ge(value_ready, c)
                for src, dst in chunk_parts(c):
                    for k in range(4):
                        last = nc.vector.tensor_scalar(dst[:, :, :, k], src, 4 * k, 7, ALU.logical_shift_right,
                                                       ALU.bitwise_and)
                last.then_inc(codes, 1)

            def magnitudes(c):
                dve.wait_ge(codes, c + 1)
                dve.wait_ge(biased, c + 1)
                link(nc.vector.tensor_scalar(mag16, mag16, float(0x3800), float(0x7000), ALU.mult, ALU.min))
                link(nc.vector.tensor_tensor(value16, mag16, value16, ALU.min))

            def signs(c):
                for src, dst in chunk_parts(c):
                    for k in range(4):
                        last = nc.vector.tensor_scalar(dst[:, :, :, k], src, 12 - 4 * k, 0x8000,
                                                       ALU.logical_shift_left, ALU.bitwise_and)
                link(last)
                value32 = value16.bitcast(U32)
                nc.vector.tensor_tensor(value32, value32, mag[:, :], ALU.bitwise_or).then_inc(value_ready, 1)

            def scaled_down(c):
                dve.wait_ge(value_ready, c + 1)
                if c:
                    dve.wait_ge(d_fill, c)
                nc.vector.tensor_tensor(w32.rearrange("p (k n) -> p k n", n=P),
                                        value16.bitcast(F16)[:, 8 * P:12 * P].rearrange("p (k n) -> p k n", n=P),
                                        sc_d[:, :, c].unsqueeze(2).broadcast_to([P, KT, P]), ALU.mult)\
                    .then_inc(w32_ready, 1)

            def down_low(c, bank):
                dve.wait_ge(dhi_done, c + 1)
                nc.vector.tensor_tensor(wd_lo[:, c, :], bank[:, :], wd_hi[:, c, :].bitcast(F32), ALU.subtract)\
                    .then_inc(dlo_done, 1)

            for t in range(TT):
                bn(0, t)
            stats_complete(0)
            aggregate(0)
            for t in range(TT):
                norm(0, t)
            dve.wait_ge(d_gu, 16)
            dve.wait_ge(d_down, 16)
            magnitude_codes(0)
            dve.wait_ge(d_scales, 32)
            dve.wait_ge(d_wsa, 32)
            nc.vector.tensor_copy(d32, raw_d).then_inc(scale_cast, 1)
            xt_low(0, 0, 0, x0_bank[0])
            magnitudes(0)
            signs(0)
            dve.wait_ge(scale_fill, 2)
            nc.vector.tensor_copy(sc_d[:, :, :],
                                  ring[1][:, 0:KT * 16].rearrange("p (k g) -> p k g", g=16)[:, :, 0:STEPS])\
                .then_inc(dq, 1)
            links[0] += 1
            raw = ring[0][:, :].bitcast(F16)[:, 0:2 * STEPS * KT].rearrange("p (t k) -> p t k", k=KT)
            nc.vector.tensor_scalar(sc_gu[:, 0:STEPS, :], raw[:, 0:STEPS, :], 1.0 / XSCALE, None, ALU.mult)
            nc.vector.tensor_scalar(sc_gu[:, STEPS:2 * STEPS, :], raw[:, STEPS:2 * STEPS, :], 0.5 / XSCALE, None,
                                    ALU.mult).then_inc(scale_done, 2)
            for k in range(1, KT):
                xt_low(0, 0, k, x0_bank[k])
            dve.wait_ge(dq, links[0])
            scaled_down(0)
            magnitude_codes(1)
            dve.wait_ge(wsa_split, 1)
            nc.vector.tensor_tensor(wsa_lo[:, :, :], wsa32, wsa_hi[:, :, :].bitcast(F32), ALU.subtract)\
                .then_inc(wsa_done, 1)

            def wo_low(k):
                dve.wait_ge(wohi_done, k + 1)
                nc.vector.tensor_tensor(wo_lo[:, k, :], wo_bank[k][:, :], wo_hi[:, k, :].bitcast(F32),
                                        ALU.subtract).then_inc(wolo_done, 1)

            wo_low(0)
            magnitudes(1)
            wo_low(1)
            signs(1)
            for k in range(2, KT):
                wo_low(k)
            down_low(0, aux)
            scaled_down(1)

            def iteration(b, par, work, prev, more):
                def evac(i, u):
                    sp = (par + i) % 2
                    dve.wait_ge(act_evac, NU // 2 * b + KT * i + u // 2 + 1)
                    dve.wait_ge(unit_done, NU * b + UNITS * i + u + 1)
                    dst = acc[:, {1: sp, 3: 4, 5: 2 + sp, 7: 5}[u], :]
                    t = i if u < KT else STEPS + i
                    nc.vector.scalar_tensor_tensor(dst, ring[SLOTS_OF[UNITS * i + u]][:, :],
                                                   sc_gu[:, t, u % KT:u % KT + 1], dst, ALU.mult, ALU.add)\
                        .then_inc(dve_evac, 1)

                def hidden(i):
                    dst = acc[:, 2 + (par + i - 1) % 2, :]
                    dve.wait_ge(m_done, STEPS * b + i)
                    dve.wait_ge(tanh_done, STEPS * b + i)
                    nc.vector.scalar_tensor_tensor(dst, th[:, :], 1.0, dst, ALU.add, ALU.mult).then_inc(h_done, 1)
                    dve.wait_ge(h_done, STEPS * b + i)
                    wait(dve, down_done, 44 * b + 4 * i - 8)
                    nc.vector.tensor_copy(h_bf[:, h_slot(i - 1), :], dst).then_inc(hbf_done, 1)

                def aux_read(index):
                    slot = aux_slot(index, more)
                    if slot is None:
                        return
                    kind, n = slot
                    if kind == "T":
                        xt_low(b + 1, 1 - par, n, aux)
                    elif kind == "SA":
                        dve.wait_ge(sa_hi, 2 * b + 2)
                        for (hi, lo), rows in (((s_hi, s_lo), slice(0, RANK)), ((a_hi, a_lo), slice(RANK, 2 * RANK))):
                            nc.vector.tensor_tensor(lo[:, :], aux[rows, :], hi[:, :].bitcast(F32), ALU.subtract)\
                                .then_inc(sa_lo, 1)
                    elif kind == "V":
                        dve.wait_ge(vhi_done, 4 * b + n + 1)
                        nc.vector.tensor_tensor(v_lo[:, n, :], aux[:, :], v_hi[:, n, :].bitcast(F32), ALU.subtract)\
                            .then_inc(vlo_done, 1)
                    elif kind == "E":
                        dve.wait_ge(ready[kind], 4 * b + n + 1)
                        nc.vector.reduce_max(smax[:, n:n + 1], aux[:, 0:(n + 1) * P], AX.X).then_inc(max_done, 1)
                        dve.wait_ge(max_done, 4 * b + n + 1)
                        nc.vector.tensor_scalar(nbias[:, n:n + 1], smax[:, n:n + 1], -QSCALE, None, ALU.mult)\
                            .then_inc(nb_done, 1)
                    elif kind == "F":
                        dve.wait_ge(pthi_done, 4 * b + n + 1)
                        cols = (n + 1) * P
                        nc.vector.tensor_tensor(pt_lo[:, 0:cols], aux[:, 0:cols], pt_hi[:, 0:cols].bitcast(F32),
                                                ALU.subtract).then_inc(ptlo_done, 1)
                    else:
                        dve.wait_ge(exp_done, 4 * b + n + 1)
                        nc.vector.reciprocal(rinv[:, n:n + 1], rsum[:, n:n + 1]).then_inc(rinv_done, 1)
                        dve.wait_ge(rinv_done, 4 * b + n + 1)
                        dve.wait_ge(ready[kind], 4 * b + n + 1)
                        wait(dve, fa_done, 4 * (b - 1) + n + 1)
                        nc.vector.scalar_tensor_tensor(att[:, n, :], aux[:, :], rinv[:, n:n + 1], bias[:, :],
                                                       ALU.mult, ALU.add).then_inc(att_done, 1)

                def layer_norm_part(i):
                    if i == 4:
                        for t in range(TT):
                            bn(b + 1, t)
                        stats_complete(b + 1)
                        aggregate(b + 1)
                    if i == 6:
                        for t in range(TT):
                            norm(b + 1, t)

                def gated(t):
                    k = 4 * (b - 1) + t
                    dst = fin[:, t, :]
                    dve.wait_ge(ytanh_done, k + 1)
                    nc.vector.scalar_tensor_tensor(dst, dst, r2[:, t:t + 1], att[:, t, :], ALU.mult,
                                                   ALU.mult).then_inc(fa_done, 1)
                    dve.wait_ge(fa_done, k + 1)
                    nc.vector.scalar_tensor_tensor(dst, fin[:, 6, :], 1.0, dst, ALU.add, ALU.mult)\
                        .then_inc(fb_done, 1)

                if not work:
                    hidden(0)
                    for t in range(TT):
                        gated(t)
                    return
                for i in range(STEPS):
                    if is_first(b):
                        c = valued_chunk(b, i)
                        evac(i, 1)
                        if stored_chunk(b, i) is not None:
                            down_low(stored_chunk(b, i), aux)
                        if c is not None:
                            magnitude_codes(c)
                        evac(i, 3)
                        aux_read(2 * i)
                        if c is not None:
                            magnitudes(c)
                        if i:
                            hidden(i)
                        evac(i, 5)
                        if c is not None:
                            signs(c)
                        aux_read(2 * i + 1)
                        evac(i, 7)
                        if c is not None:
                            scaled_down(c)
                        layer_norm_part(i)
                        continue
                    evac(i, 1)
                    aux_read(2 * i)
                    if more and i == 6:
                        norm(b + 1, 2)
                        norm(b + 1, 3)
                    evac(i, 3)
                    if i or prev:
                        hidden(i)
                    evac(i, 5)
                    aux_read(2 * i + 1)
                    if more and i == 3:
                        stats_complete(b + 1)
                    evac(i, 7)
                    if more:
                        if i in (1, 2):
                            bn(b + 1, 2 * i - 2)
                            bn(b + 1, 2 * i - 1)
                        if i == 3:
                            aggregate(b + 1)
                        if i == 5:
                            norm(b + 1, 0)
                            norm(b + 1, 1)
                    if prev and i in (3, 4, 6, 8):
                        gated((3, 4, 6, 8).index(i))

            dve.wait_ge(d_bo, 16)
            run_batches(dve, iteration)

        @block.gpsimd
        def _(pool):
            nc.gpsimd.memset(ident[:, :], 0.0)
            nc.gpsimd.memset(ident16[:, :], 0.0)
            nc.gpsimd.memset(identb[:, :], 0.0)
            nc.gpsimd.memset(maskb[:, :], 0.0)
            for n, value in enumerate(CONSTS):
                last = nc.gpsimd.memset(const[:, n, :], value)
            last.then_inc(const_made, 1)
            pool.wait_ge(const_made, 1)
            for m in (ident, ident16, identb):
                nc.gpsimd.affine_select(out=m[:, :], in_=m[:, :], compare_op=ALU.not_equal, fill=1.0, base=0,
                                        pattern=[[-1, P]], channel_multiplier=1).then_inc(const_made, 1)
            nc.gpsimd.affine_select(out=maskb[:, :], in_=maskb[:, :], compare_op=ALU.is_ge, fill=NEG, base=0,
                                    pattern=[[-1, P]], channel_multiplier=1).then_inc(const_made, 1)

            def rstd_of(B):
                pool.wait_ge(aggr_done, 4 * B + 4)
                wait(pool, xn_done, 4 * B)
                nc.gpsimd.tensor_tensor(vare[:, :], mv[:, :, 1], const[:, 1, :], ALU.add)\
                    .then_inc(var_done, 1)
                pool.wait_ge(var_done, B + 1)
                nc.gpsimd.tensor_tensor(rstd[:, :], vare[:, :], const[:, 0, :], ALU.pow).then_inc(rstd_done, 1)

            rstd_of(0)

            def iteration(b, par, work, prev, more):
                def gate_sum(i):
                    pool.wait_ge(dve_evac, NU // 2 * b + KT * i + 2)
                    dst = acc[:, (par + i) % 2, :]
                    nc.gpsimd.tensor_tensor(dst, dst, acc[:, 4, :], ALU.add).then_inc(gsum, 1)

                def up_sum_and_product(i):
                    G = STEPS * b + i
                    sp = (par + i - 1) % 2
                    dst = acc[:, 2 + sp, :]
                    pool.wait_ge(dve_evac, NU // 2 * b + KT * i)
                    nc.gpsimd.tensor_tensor(dst, dst, acc[:, 5, :], ALU.add).then_inc(usum, 1)
                    pool.wait_ge(usum, G)
                    nc.gpsimd.tensor_tensor(dst, dst, acc[:, sp, :], ALU.mult).then_inc(m_done, 1)

                def hidden_low(i):
                    pool.wait_ge(hhi_done, STEPS * b + i)
                    s = h_slot(i - 1)
                    nc.gpsimd.tensor_tensor(h_lo[:, s, :], acc[:, 2 + (par + i - 1) % 2, :],
                                            h_hi[:, s, :].bitcast(F32), ALU.subtract).then_inc(hlo_done, 1)

                def rms(t):
                    k = 4 * (b - 1) + t
                    pool.wait_ge(sq_done, k + 1)
                    nc.gpsimd.tensor_tensor(msq[:, 0, t:t + 1], ssq[:, t:t + 1], const[:, 2, 0:1], ALU.mult)\
                        .then_inc(msq_done, 1)
                    pool.wait_ge(msq_done, 2 * k + 1)
                    nc.gpsimd.tensor_tensor(msq[:, 1, t:t + 1], msq[:, 0, t:t + 1], const[:, 3, 0:1], ALU.add)\
                        .then_inc(msq_done, 1)
                    pool.wait_ge(msq_done, 2 * k + 2)
                    nc.gpsimd.tensor_tensor(r2[:, t:t + 1], msq[:, 1, t:t + 1], const[:, 0, 0:1], ALU.pow)\
                        .then_inc(r2_done, 1)

                def add_x(t):
                    k = 4 * (b - 1) + t
                    pool.wait_ge(fb_done, k + 1)
                    pool.wait_ge(xr_loaded[t % 2], 16 * (2 * (b - 1) + t // 2 + 1))
                    dst = fin[:, t, :]
                    nc.gpsimd.tensor_tensor(dst, dst, fin[:, 4 + t % 2, :], ALU.add).then_inc(add_done, 1)

                if not work:
                    up_sum_and_product(0)
                    hidden_low(0)
                    for t in range(TT):
                        rms(t)
                        add_x(t)
                    return
                for i in range(STEPS):
                    if i or prev:
                        up_sum_and_product(i)
                    if more and i == (6 if is_first(b) else 4):
                        rstd_of(b + 1)
                    if prev and i in (3, 4, 5, 6):
                        rms(i - 3)
                    gate_sum(i)
                    if i or prev:
                        hidden_low(i)
                    if prev and i in (4, 5, 7, 9):
                        add_x((4, 5, 7, 9).index(i))

            run_batches(pool, iteration)


_INS = ['L0_attn_x', 'L0_attn_Ws', 'L0_attn_Wa', 'L0_attn_Wo', 'L0_attn_bo', 'L0_ffn_gate_up_packed',
        'L0_ffn_gate_up_scales', 'L0_ffn_down_packed', 'L0_ffn_down_scales']


def kernel(**inputs):
    import numpy as _np
    import concourse.bacc as _bacc
    from concourse import mybir as _mybir
    from concourse.bass_utils import run_bass_kernel_spmd as _run

    nc = _bacc.Bacc("TRN2", target_bir_lowering=False, num_devices=1)
    arrays, args = {}, []
    for name in _INS:
        a = _np.ascontiguousarray(inputs[name])
        arrays[f"in_{name}_dram"] = a
        args.append(nc.dram_tensor(f"in_{name}_dram", a.shape, _mybir.dt.from_np(a.dtype), kind="ExternalInput").ap())
    shape = arrays["in_L0_attn_x_dram"].shape
    out = nc.dram_tensor("out_0_dram", shape, _mybir.dt.from_np(_np.dtype("float32")), kind="ExternalOutput").ap()
    gated_attention_ffn(nc, *args, out)
    r = _run(nc, [arrays], core_ids=[0])
    return r.results[0]["out_0_dram"]
```

```python
from contextlib import ExitStack

import concourse.bass as bass
from concourse import mybir

F32 = mybir.dt.float32
F32R = mybir.dt.float32r
F16 = mybir.dt.float16
BF16 = mybir.dt.bfloat16
U16 = mybir.dt.uint16
U32 = mybir.dt.int32
ALU = mybir.AluOpType
ACT = mybir.ActivationFunctionType
AX = mybir.AxisListType

AUX_SLOTS = [("SA", 0), ("V", 0), ("V", 1), ("E", 0), ("V", 2), ("E", 1), ("F", 0), ("V", 3), ("G", 0), ("F", 1),
             ("E", 2), ("G", 1), ("F", 2), ("E", 3), ("G", 2), ("T", 0), ("F", 3), ("T", 1), ("G", 3), ("T", 2),
             ("T", 3), None]


TANH_STEPS = (3, 4, 6, 8)
GATED_STEPS = (4, 5, 7, 9)
ADD_X_STEPS = (6, 8, 9, 10)


def gated_attention_ffn(nc, x, Ws, Wa, Wo, bo, gu_packed, gu_scales, down_packed, down_scales, out):
    BATCH, SEQ, HID = x.shape
    RANK = Ws.shape[1]
    INNER = gu_packed.shape[0] // 2
    P = 128
    TT = SEQ // P
    KT = HID // P
    STEPS = INNER // P
    UNITS = 2 * KT
    NU = UNITS * STEPS
    QSCALE = float(RANK) ** -0.5
    XSCALE = 1024.0
    LN_EPS, RMS_EPS = 1e-5, 1e-6
    NEG = -3.0e38
    WORDS = HID // 8
    DWORDS = INNER // 8

    x_v = x.rearrange("b (t p) h -> b p t h", p=P)
    out_v = out.rearrange("b (t p) h -> b p t h", p=P)

    ctx = ExitStack()
    with ctx:
        def sb(name, shape, dt):
            return ctx.enter_context(nc.sbuf_tensor(name, shape, dt))

        def pb(name, shape, dt):
            return ctx.enter_context(nc.psum_tensor(name, shape, dt))

        def sem(name):
            return ctx.enter_context(nc.semaphore(name))

        w_gu = sb("w_gu", [P, KT, 2 * INNER], F16)
        wd_hi = sb("wd_hi", [P, STEPS, HID], F32R)
        wd_lo = sb("wd_lo", [P, STEPS, HID], BF16)
        wo_hi = sb("wo_hi", [P, KT, HID], F32R)
        wo_lo = sb("wo_lo", [P, KT, HID], F32R)
        wsa_hi = sb("wsa_hi", [P, KT, 2 * RANK], F32R)
        wsa_lo = sb("wsa_lo", [P, KT, 2 * RANK], F32R)
        sc_gu = sb("sc_gu", [P, 2 * STEPS, KT], F32)
        sc_d = sb("sc_d", [P, KT, STEPS], F32)
        bias = sb("bias", [P, HID], F32)
        ident = sb("ident", [P, P], F32)
        ident16 = sb("ident16", [P, P], F16)
        identb = sb("identb", [P, P], BF16)
        maskb = sb("maskb", [P, P], BF16)
        const = sb("const", [P, 4, TT], F32)
        CONSTS = (-0.5, LN_EPS, 4.0 / HID, 4.0 * RMS_EPS)
        xn = sb("xn", [P, TT, HID], F32)
        xt_hi = sb("xt_hi", [P, KT, SEQ], F32R)
        xt_lo = sb("xt_lo", [P, KT, SEQ], F32R)
        x16 = sb("x16", [P, 2, 2, KT, SEQ], F16)
        state = sb("state", [2 * RANK, SEQ], F32R)
        action = sb("action", [2 * RANK, SEQ], F32R)
        a_lo = sb("a_lo", [RANK, SEQ], F32R)
        v_hi = sb("v_hi", [P, TT, HID], F32R)
        v_lo = sb("v_lo", [P, TT, HID], F32R)
        prob = sb("prob", [P, 2, SEQ], F32)
        pt_hi = sb("pt_hi", [P, SEQ], F32R)
        pt_lo = sb("pt_lo", [P, SEQ], F32R)
        att = sb("att", [P, TT, HID], F32)
        acc = sb("acc", [P, 6, SEQ], F32)
        th = sb("th", [P, SEQ], F32)
        h_hi = sb("h_hi", [P, 3, SEQ], F32R)
        h_lo = sb("h_lo", [P, 3, SEQ], F32R)
        h_bf = sb("h_bf", [P, 3, SEQ], BF16)
        fin = sb("fin", [P, 7, HID], F32)
        junk = sb("junk", [P, HID], BF16)
        mag = sb("mag", [P, 3 * SEQ // 2], U32)
        stats = sb("stats", [P, TT, 6], F32)
        mv = sb("mv", [P, TT, 2], F32)
        vare = sb("vare", [P, TT], F32)
        rstd = sb("rstd", [P, TT], F32)
        smax = sb("smax", [P, TT], F32)
        nbias = sb("nbias", [P, TT], F32)
        rsum = sb("rsum", [P, TT], F32)
        rinv = sb("rinv", [P, TT], F32)
        ssq = sb("ssq", [P, TT], F32)
        msq = sb("msq", [P, 2, TT], F32)
        r2 = sb("r2", [P, TT], F32)

        y = [pb(f"y{t}", [P, HID], F32) for t in range(TT)]
        ring = [pb(f"ring{n}", [P, SEQ], F32) for n in range(3)]
        aux = pb("aux", [P, SEQ], F32)

        def ring_slot(n):
            return n % 3 if n < NU - 1 else 1

        SLOTS_OF = [ring_slot(n) for n in range(NU)]

        def ring_before(n):
            m = n - 1
            while SLOTS_OF[m % NU] != SLOTS_OF[n]:
                m -= 1
            return m

        fin_w = fin[:, :, :].rearrange("p a b -> p (a b)").bitcast(U32)
        pk_gu = fin_w[:, 0:2 * STEPS * WORDS].rearrange("p (t w) -> p t w", w=WORDS)
        at_d = 2 * STEPS * WORDS
        pk_d = fin_w[:, at_d:at_d + KT * DWORDS].rearrange("p (t w) -> p t w", w=DWORDS)
        at_v = at_d + KT * DWORDS
        CHUNK = (2 * KT + KT) * P
        value16 = fin_w[:, at_v:at_v + CHUNK // 2].bitcast(U16)
        w32 = fin_w[:, at_v + CHUNK // 2:at_v + CHUNK // 2 + HID].bitcast(F32)
        mag16 = mag[:, :].bitcast(U16)
        x16_1 = x16[:, 1, :, :, :].rearrange("p a b c -> p (a b c)")
        raw_gu = x16_1[0:KT, 0:2 * INNER]
        raw_d = x16_1[0:STEPS, 2 * INNER:2 * INNER + HID]
        wsa32 = prob[:, 0, :].rearrange("p (k r) -> p k r", k=KT)
        d32 = prob[0:STEPS, 1, :]

        d_wsa, d_scales, d_ahead, d_gu, d_wo, d_down, d_bo = (
            sem(n) for n in ("d_wsa", "d_scales", "d_ahead", "d_gu", "d_wo", "d_down", "d_bo"))
        x_first = [sem(f"x_first{t}") for t in range(TT)]
        const_made = sem("const_made")
        scale_cast = sem("scale_cast")
        scale_fill, scale_done = sem("scale_fill"), sem("scale_done")
        wsa_split, wsa_done = sem("wsa_split"), sem("wsa_done")
        wo_fill, wohi_done, wolo_done = sem("wo_fill"), sem("wohi_done"), sem("wolo_done")
        codes, biased, dq = sem("codes"), sem("biased"), sem("dq")
        value_ready, w32_ready = sem("value_ready"), sem("w32_ready")
        gu_fill, gu_done = sem("gu_fill"), sem("gu_done")
        d_fill, dhi_done, dlo_done = sem("d_fill"), sem("dhi_done"), sem("dlo_done")
        xin_loaded = sem("xin_loaded")
        bn_done, aggr_done, var_done, rstd_done, xn_done = (
            sem(n) for n in ("bn_done", "aggr_done", "var_done", "rstd_done", "xn_done"))
        unit_done, act_evac, dve_evac = sem("unit_done"), sem("act_evac"), sem("dve_evac")
        gsum, usum, m_done, tanh_done, h_done, hbf_done, hhi_done, hlo_done, down_done = (
            sem(n) for n in ("gsum", "usum", "m_done", "tanh_done", "h_done", "hbf_done", "hhi_done", "hlo_done",
                             "down_done"))
        ready = {k: sem(f"{k}_ready") for k in ("SA", "V", "E", "F", "G", "T")}
        action_twice = sem("action_twice")
        sa_hi, sa_lo, vhi_done, vlo_done, max_done, nb_done, exp_done, pthi_done, ptlo_done, rinv_done, att_done = (
            sem(n) for n in ("sa_hi", "sa_lo", "vhi_done", "vlo_done", "max_done", "nb_done", "exp_done", "pthi_done",
                             "ptlo_done", "rinv_done", "att_done"))
        xthi_done, xtlo_done = sem("xthi_done"), sem("xtlo_done")
        sq_done, msq_done, r2_done, ytanh_done, fa_done, fb_done, add_done = (
            sem(n) for n in ("sq_done", "msq_done", "r2_done", "ytanh_done", "fa_done", "fb_done", "add_done"))
        xr_loaded = [sem(f"xr_loaded{n}") for n in range(2)]
        stored = [sem(f"stored{n}") for n in range(TT)]
        ycopy_done = sem("ycopy_done")

        def wait(eng, s, value):
            if not isinstance(value, int) or value > 0:
                eng.wait_ge(s, value)

        def first_batch():
            return 0, 0, True, False, True

        def in_loop(pair, k):
            return 2 * pair + k, k % 2, True, True, True

        def last_batch():
            return BATCH - 1, (BATCH - 1) % 2, True, True, False

        def drain():
            return BATCH, BATCH % 2, False, True, False

        PAIRS = (BATCH - 2) // 2

        def run_batches(eng, iteration):
            iteration(*first_batch())
            with eng.Fori(0, PAIRS) as pair:
                iteration(*in_loop(pair, 1))
                iteration(*in_loop(pair, 2))
            iteration(*last_batch())
            iteration(*drain())

        def aux_slot(index, b, more):
            slot = AUX_SLOTS[index]
            absent = slot is None or (slot[0] == "SA" and is_first(b)) or (slot[0] == "T" and not more)
            return None if absent else slot

        def is_short(index, b, more):
            slot = aux_slot(index, b, more)
            return slot is None or slot[0] in ("E", "F", "T")

        def h_slot(i):
            return i % STEPS % 3

        def is_first(b):
            return isinstance(b, int) and b == 0

        def stored_chunk(b, i):
            return i + 1 if is_first(b) and i + 1 < STEPS else None

        def valued_chunk(b, i):
            return i + 2 if is_first(b) and i + 2 < STEPS else None

        x0_bank = wo_bank = y

        block = ctx.enter_context(nc.Block())

        @block.sync
        def _(sp):
            for t in range(TT):
                sp.dma_start(xn[:, t, :], x_v[0][:, t, :]).then_inc(x_first[t], 16)
            sp.dma_start(raw_gu, gu_scales).then_inc(d_scales, 16)
            sp.dma_start(raw_d, down_scales).then_inc(d_scales, 16)
            sp.dma_start(att[:, :, :], Wo.rearrange("(t p) h -> p t h", p=P)).then_inc(d_wo, 16)
            sp.dma_start(bias[:, :], bo.partition_broadcast(P)).then_inc(d_bo, 16)

            def iteration(b, par, work, prev, more):
                if more:
                    sp.wait_ge(ready["T"], 4 * b + 4)
                    sp.dma_start(xn[:, :, :], x_v[b + 1]).then_inc(xin_loaded, 16)
                if prev:
                    for t in range(TT):
                        wait(sp, add_done, 4 * (b - 1) + max(t - 1, 0))
                        sp.wait_ge(dlo_done, STEPS)
                        sp.dma_start(fin[:, 4 + t % 2, :], x_v[b - 1][:, t, :])\
                          .then_inc(xr_loaded[t % 2], 16)
                        if t >= 1:
                            sp.wait_ge(add_done, 4 * (b - 1) + t)
                            sp.dma_start(out_v[b - 1][:, t - 1, :], fin[:, t - 1, :])\
                              .then_inc(stored[t - 1], 16)
                    sp.wait_ge(add_done, 4 * (b - 1) + TT)
                    sp.dma_start(out_v[b - 1][:, TT - 1, :], fin[:, TT - 1, :])\
                      .then_inc(stored[TT - 1], 16)

            run_batches(sp, iteration)
            for t in range(TT):
                sp.wait_ge(stored[t], 16 * BATCH)

        @block.tensor
        def _(pe):
            pe.wait_ge(const_made, 5)
            for t in range(TT):
                pe.wait_ge(xn_done, t + 1)
                for k in range(KT):
                    last = nc.tensor.transpose(x0_bank[k][:, t * P:(t + 1) * P], xn[:, t, k * P:(k + 1) * P],
                                               ident[:, :])
                    if t == TT - 1:
                        last.then_inc(ready["T"], 1)
            pe.wait_ge(d_scales, 32)
            for t in range(2 * STEPS):
                last = nc.tensor.transpose(ring[0][:, :].bitcast(F16)[:, t * KT:(t + 1) * KT],
                                           raw_gu[:, t * P:(t + 1) * P], ident16[0:KT, 0:KT])
            last.then_inc(scale_fill, 1)
            pe.wait_ge(scale_cast, 1)
            for k in range(KT):
                last = nc.tensor.transpose(ring[1][:, k * 16:k * 16 + STEPS], d32[:, k * P:(k + 1) * P],
                                           ident[0:STEPS, 0:STEPS])
            last.then_inc(scale_fill, 1)
            def transpose_gate_up(c, bank):
                pe.wait_ge(value_ready, c + 1)
                values = value16.bitcast(F16)
                for n in range(2 * KT):
                    last = nc.tensor.transpose(bank[:, :].bitcast(F16)[:, n * P:(n + 1) * P],
                                               values[:, n * P:(n + 1) * P], ident16[:, :])
                last.then_inc(gu_fill, 1)

            def transpose_down(c, bank):
                pe.wait_ge(w32_ready, c + 1)
                for k in range(KT):
                    last = nc.tensor.transpose(bank[:, k * P:(k + 1) * P], w32[:, k * P:(k + 1) * P], ident[:, :])
                last.then_inc(d_fill, 1)

            transpose_gate_up(0, ring[2])
            transpose_down(0, aux)
            pe.wait_ge(d_wo, 16)
            for k in range(KT):
                pe.wait_ge(xtlo_done, 2 * k + 2)
                for t in range(KT):
                    last = nc.tensor.transpose(wo_bank[k][:, t * P:(t + 1) * P],
                                               att[:, t, k * P:(k + 1) * P], ident[:, :])
                last.then_inc(wo_fill, 1)

            def state_action(k):
                pairs = ((wsa_hi, xt_hi), (wsa_hi, xt_lo), (wsa_lo, xt_hi))
                return [(w[:, k, :], v[:, k, :]) for w, v in pairs]

            pe.wait_ge(wsa_done, 1)
            pe.wait_ge(gu_done, 1)
            for k in range(KT):
                for n, (w, v) in enumerate(state_action(k)):
                    last = nc.tensor.matmul(ring[2][:, :], w, v, start=(k == 0 and n == 0),
                                            stop=(k == KT - 1 and n == 2))
            last.then_inc(ready["SA"], 1)

            def iteration(b, par, work, prev, more):
                def unit(i, u):
                    n, k = UNITS * i + u, u % KT
                    m = ring_before(n)
                    wait(pe, act_evac if m % 2 == 0 else dve_evac, NU // 2 * b + (m - m % 2) // 2 + 1)
                    if i == 0 and u < KT:
                        pe.wait_ge(xtlo_done, 8 * b + 2 * u + 2)
                    if is_first(b) and i == 0 and u == 2:
                        pe.wait_ge(sa_lo, 2)
                    if is_first(b) and u == 0:
                        pe.wait_ge(gu_done, i + 1)
                        pe.wait_ge(scale_done, 2)
                    o = (i if u < KT else STEPS + i) * P
                    for part in range(2):
                        last = nc.tensor.matmul(ring[SLOTS_OF[n]][:, :], w_gu[:, k, o:o + P], x16[:, par, part, k, :],
                                                start=(part == 0), stop=(part == 1))
                    last.then_inc(unit_done, 1)

                def down(i, t):
                    if i < 2 and not prev:
                        return
                    ii = (i - 2) % STEPS
                    hs = h_slot(ii)
                    if t == 0:
                        pe.wait_ge(hlo_done, STEPS * b + i - 1)
                        pe.wait_ge(hbf_done, STEPS * b + i - 1)
                    if is_first(b) and t == 0:
                        pe.wait_ge(dlo_done, ii + 1)
                    if ii == 0:
                        wait(pe, ycopy_done, 4 * (b - 1) + t + 1)
                    tt = slice(t * P, (t + 1) * P)
                    nc.tensor.matmul(y[t][:, :], h_hi[:, hs, tt], wd_hi[:, ii, :], start=(ii == 0), stop=False)
                    nc.tensor.matmul(y[t][:, :], h_lo[:, hs, tt], wd_hi[:, ii, :], start=False, stop=False)
                    nc.tensor.matmul(y[t][:, :], h_bf[:, hs, tt], wd_lo[:, ii, :], start=False,
                                     stop=(ii == STEPS - 1)).then_inc(down_done, 1)

                def aux_bank_free(index, after_chunk=True):
                    if is_first(b) and index == 1:
                        pe.wait_ge(dlo_done, 2)
                        return
                    if after_chunk and index % 2 == 0 and (index == 0 or stored_chunk(b, index // 2) is not None)\
                            and is_first(b):
                        pe.wait_ge(dlo_done, index // 2 + 2)
                        return
                    index -= 1
                    while index >= 0 and aux_slot(index, b, more) is None:
                        index -= 1
                    kind, n = AUX_SLOTS[index] if index >= 0 else ("T", 3)
                    if kind == "T":
                        pe.wait_ge(xtlo_done, 8 * b + 2 * n + 2 + (8 if index >= 0 else 0))
                    elif kind == "SA":
                        pe.wait_ge(sa_lo, 2 * b + 2)
                    else:
                        pe.wait_ge({"V": vlo_done, "E": exp_done, "F": ptlo_done, "G": att_done}[kind], 4 * b + n + 1)

                def aux_work(index):
                    slot = aux_slot(index, b, more)
                    if slot is None:
                        yield
                        yield
                        return
                    kind, n = slot
                    aux_bank_free(index)
                    if is_first(b) and kind == "V":
                        pe.wait_ge(wolo_done, KT)
                    if kind in ("SA", "V"):
                        products = []
                        for k in range(KT):
                            if kind == "SA":
                                products += state_action(k)
                            else:
                                tt = slice(n * P, (n + 1) * P)
                                pairs = ((xt_hi, wo_hi), (xt_lo, wo_hi), (xt_hi, wo_lo))
                                products += [(v[:, k, tt], w[:, k, :]) for v, w in pairs]
                        half = len(products) // 2
                        for m, (lhs, rhs) in enumerate(products):
                            if m == half:
                                yield
                            last = nc.tensor.matmul(aux[:, :], lhs, rhs, start=(m == 0), stop=(m == len(products) - 1))
                    elif kind == "E":
                        if n == 0:
                            pe.wait_ge(sa_lo, 2 * b + 2)
                            pe.wait_ge(action_twice, b + 1)
                        cols = max(2 * P, (n + 1) * P)
                        q = slice(n * P, (n + 1) * P)
                        nc.tensor.matmul(aux[:, 0:cols], state[:, q], action[:, 0:cols], start=True, stop=False)
                        nc.tensor.matmul(aux[:, 0:cols], state[0:RANK, q], a_lo[:, 0:cols], start=False, stop=False)
                        nc.tensor.matmul(aux[:, q], identb[:, :], maskb[:, :], start=False, stop=True)\
                            .then_inc(ready[kind], 1)
                        yield
                        yield
                        return
                    elif kind == "F":
                        pe.wait_ge(exp_done, 4 * b + n + 1)
                        for j in range(n + 1):
                            last = nc.tensor.transpose(aux[:, j * P:(j + 1) * P], prob[:, n % 2, j * P:(j + 1) * P],
                                                       ident[:, :])
                        last.then_inc(ready[kind], 1)
                        yield
                        yield
                        return
                    elif kind == "G":
                        pe.wait_ge(ptlo_done, 4 * b + n + 1)
                        if n == 0 or n == 3:
                            pe.wait_ge(vlo_done, 4 * b + n + 1)
                        products = []
                        for j in range(n + 1):
                            jj = slice(j * P, (j + 1) * P)
                            products += [(pt_hi[:, jj], v_hi[:, j, :]), (pt_lo[:, jj], v_hi[:, j, :]),
                                         (pt_hi[:, jj], v_lo[:, j, :])]
                        half = len(products) // 2
                        for m, (lhs, rhs) in enumerate(products):
                            if m == half:
                                yield
                            last = nc.tensor.matmul(aux[:, :], lhs, rhs, start=(m == 0), stop=(m == len(products) - 1))
                    else:
                        pe.wait_ge(xn_done, 4 * (b + 1) + 4)
                        for t in range(TT):
                            last = nc.tensor.transpose(aux[:, t * P:(t + 1) * P], xn[:, t, n * P:(n + 1) * P],
                                                       ident[:, :])
                        last.then_inc(ready[kind], 1)
                        yield
                        yield
                        return
                    last.then_inc(ready[kind], 1)
                    yield

                if not work:
                    for i in range(2):
                        for t in range(TT):
                            down(i, t)
                    return
                for i in range(STEPS):
                    first, second = aux_work(2 * i), aux_work(2 * i + 1)
                    if is_first(b):
                        c = stored_chunk(b, i)
                        unit(i, 0)
                        unit(i, 1)
                        unit(i, 2)
                        if c is not None:
                            if i:
                                aux_bank_free(2 * i, False)
                            else:
                                pe.wait_ge(dlo_done, 1)
                            transpose_gate_up(c, aux)
                        down(i, 0)
                        unit(i, 3)
                        down(i, 1)
                        if c is not None:
                            pe.wait_ge(gu_done, c + 1)
                            transpose_down(c, aux)
                        unit(i, 4)
                        unit(i, 5)
                        down(i, 2)
                        next(first)
                        unit(i, 6)
                        next(first)
                        unit(i, 7)
                        next(second)
                        down(i, 3)
                        next(second)
                        continue
                    unit(i, 0)
                    next(first)
                    unit(i, 1)
                    if is_short(2 * i, b, more):
                        down(i, 0)
                        unit(i, 2)
                    else:
                        next(first)
                        unit(i, 2)
                        down(i, 0)
                    unit(i, 3)
                    down(i, 1)
                    unit(i, 4)
                    next(second)
                    unit(i, 5)
                    if is_short(2 * i + 1, b, more):
                        down(i, 2)
                        unit(i, 6)
                    else:
                        next(second)
                        unit(i, 6)
                        down(i, 2)
                    if i < STEPS - 1:
                        unit(i, 7)
                        down(i, 3)
                    else:
                        down(i, 3)
                        unit(i, 7)

            run_batches(pe, iteration)

        @block.scalar
        def _(act):
            gu_words = gu_packed.rearrange("(t p) w -> p t w", p=P)
            d_words = down_packed.rearrange("(t p) w -> p t w", p=P)
            ahead = 2 * P // 8
            for at in (0, STEPS):
                act.dma_start(pk_gu[:, at:at + 2, :], gu_words[:, at:at + 2, :]).then_inc(d_ahead, 16)
            act.dma_start(pk_d[:, :, 0:ahead], d_words[:, :, 0:ahead]).then_inc(d_ahead, 16)
            for at in (0, STEPS):
                act.dma_start(pk_gu[:, at + 2:at + STEPS, :], gu_words[:, at + 2:at + STEPS, :]).then_inc(d_gu, 16)
            act.dma_start(pk_d[:, :, ahead:], d_words[:, :, ahead:]).then_inc(d_down, 16)
            act.dma_start(wsa32[:, :, 0:RANK], Ws.rearrange("(k p) r -> p k r", p=P)).then_inc(d_wsa, 16)
            act.dma_start(wsa32[:, :, RANK:2 * RANK], Wa.rearrange("(k p) r -> p k r", p=P)).then_inc(d_wsa, 16)

            def xt_high(B, par, k, bank):
                act.wait_ge(ready["T"], 4 * B + k + 1)
                if k == 0:
                    wait(act, ready["V"], 4 * B)
                nc.scalar.activation(xt_hi[:, k, :], bank[:, :], ACT.Copy).then_inc(xthi_done, 1)
                act.wait_ge(xthi_done, 8 * B + 2 * k + 1)
                nc.scalar.activation(x16[:, par, 0, k, :], xt_hi[:, k, :].bitcast(F32), ACT.Copy, scale=XSCALE)\
                    .then_inc(xthi_done, 1)

            def biased_codes(c):
                act.wait_ge(codes, c + 1)
                if c:
                    act.wait_ge(gu_fill, c)
                    act.wait_ge(w32_ready, c)
                nc.scalar.activation(value16, mag16, ACT.Copy, bias=float(0x3800), scale=float(0x200))\
                    .then_inc(biased, 1)

            def store_gate_up(c, bank):
                act.wait_ge(gu_fill, c + 1)
                dst = w_gu[:, :, :].rearrange("p k (t n) -> p t k n", t=2)[:, :, :, c * P:(c + 1) * P]
                src = bank[:, :].bitcast(F16).rearrange("p (t k n) -> p t k n", t=2, k=KT)
                nc.scalar.activation(dst, src, ACT.Copy).then_inc(gu_done, 1)

            def store_down(c, bank):
                act.wait_ge(d_fill, c + 1)
                nc.scalar.activation(wd_hi[:, c, :], bank[:, :], ACT.Copy).then_inc(dhi_done, 1)

            def state_action_high(B, bank):
                act.wait_ge(ready["SA"], B + 1)
                nc.scalar.activation(state[0:RANK, :], bank[0:RANK, :], ACT.Copy).then_inc(sa_hi, 1)
                nc.scalar.activation(action[0:RANK, :], bank[RANK:2 * RANK, :], ACT.Copy).then_inc(sa_hi, 1)

            def action_again(B):
                act.wait_ge(sa_hi, 2 * B + 2)
                nc.scalar.activation(action[RANK:2 * RANK, :], action[0:RANK, :].bitcast(F32), ACT.Copy)\
                    .then_inc(action_twice, 1)

            biased_codes(0)
            act.wait_ge(d_scales, 32)
            nc.scalar.activation(d32, raw_d, ACT.Copy).then_inc(scale_cast, 1)
            for k in range(KT):
                xt_high(0, 0, k, x0_bank[k])
            act.wait_ge(d_wsa, 32)
            nc.scalar.activation(wsa_hi[:, :, :], wsa32, ACT.Copy).then_inc(wsa_split, 1)
            store_gate_up(0, ring[2])
            store_down(0, aux)
            biased_codes(1)
            for k in range(KT):
                act.wait_ge(wo_fill, k + 1)
                nc.scalar.activation(wo_hi[:, k, :], wo_bank[k][:, :], ACT.Copy).then_inc(wohi_done, 1)
            state_action_high(0, ring[2])

            def iteration(b, par, work, prev, more):
                def evac(i, u):
                    sp = (par + i) % 2
                    G = STEPS * b + i
                    if u == 0:
                        wait(act, m_done, G - 1)
                    elif u == 2:
                        wait(act, gsum, G)
                    elif u == 4:
                        wait(act, hlo_done, G - 1)
                        wait(act, hbf_done, G - 1)
                    else:
                        wait(act, usum, G)
                    act.wait_ge(unit_done, NU * b + UNITS * i + u + 1)
                    dst = acc[:, {0: sp, 2: 4, 4: 2 + sp, 6: 5}[u], :]
                    t = i if u < KT else STEPS + i
                    nc.scalar.activation(dst, ring[SLOTS_OF[UNITS * i + u]][:, :], ACT.Copy,
                                         scale=sc_gu[:, t, u % KT:u % KT + 1]).then_inc(act_evac, 1)

                def gate_tanh(i):
                    act.wait_ge(gsum, STEPS * b + i + 1)
                    wait(act, h_done, STEPS * b + i)
                    nc.scalar.activation(th[:, :], acc[:, (par + i) % 2, :], ACT.Tanh, scale=0.5)\
                        .then_inc(tanh_done, 1)

                def hidden_high(i):
                    act.wait_ge(h_done, STEPS * b + i)
                    wait(act, down_done, 44 * b + 4 * i - 8)
                    nc.scalar.activation(h_hi[:, h_slot(i - 1), :], acc[:, 2 + (par + i - 1) % 2, :], ACT.Copy)\
                        .then_inc(hhi_done, 1)

                def hidden_bfloat(i):
                    nc.scalar.activation(h_bf[:, h_slot(i - 1), :], acc[:, 2 + (par + i - 1) % 2, :], ACT.Copy)\
                        .then_inc(hbf_done, 1)

                def aux_read(index):
                    slot = aux_slot(index, b, more)
                    if slot is None:
                        return
                    kind, n = slot
                    if kind == "T":
                        xt_high(b + 1, 1 - par, n, aux)
                        return
                    if kind == "SA":
                        wait(act, ready["E"], 4 * b)
                        state_action_high(b, aux)
                        action_again(b)
                    elif kind == "V":
                        act.wait_ge(ready[kind], 4 * b + n + 1)
                        wait(act, ready["G"], 4 * b)
                        nc.scalar.activation(v_hi[:, n, :], aux[:, :], ACT.Copy).then_inc(vhi_done, 1)
                    elif kind == "E":
                        act.wait_ge(nb_done, 4 * b + n + 1)
                        wait(act, ready["F"], 4 * b + n - 1)
                        wait(act, rinv_done, 4 * b + n - 3)
                        cols = (n + 1) * P
                        nc.scalar.activation(prob[:, n % 2, 0:cols], aux[:, 0:cols], ACT.Exp,
                                             bias=nbias[:, n:n + 1], scale=QSCALE,
                                             accum_out=rsum[:, n:n + 1]).then_inc(exp_done, 1)
                    elif kind == "F":
                        act.wait_ge(ready[kind], 4 * b + n + 1)
                        wait(act, ready["G"], 4 * b + n)
                        cols = (n + 1) * P
                        nc.scalar.activation(pt_hi[:, 0:cols], aux[:, 0:cols], ACT.Copy).then_inc(pthi_done, 1)

                def copy_y(t):
                    act.wait_ge(down_done, 44 * b + t - 3)
                    wait(act, stored[t], 16 * (b - 1))
                    nc.scalar.activation(fin[:, t, :], y[t][:, :], ACT.Copy).then_inc(ycopy_done, 1)

                def sum_of_squares(t):
                    act.wait_ge(ycopy_done, 4 * (b - 1) + t + 1)
                    wait(act, sq_done, 4 * (b - 1) + t)
                    wait(act, msq_done, 8 * (b - 1))
                    nc.scalar.activation(junk[:, :], fin[:, t, :], ACT.Square, accum_out=ssq[:, t:t + 1])\
                        .then_inc(sq_done, 1)

                def silu_tanh(t):
                    act.wait_ge(r2_done, 4 * (b - 1) + t + 1)
                    wait(act, fb_done, 4 * (b - 1) + t)
                    nc.scalar.activation(fin[:, 6, :], fin[:, t, :], ACT.Tanh, scale=r2[:, t:t + 1])\
                        .then_inc(ytanh_done, 1)

                if not work:
                    hidden_high(0)
                    for t in range(TT + 1):
                        if t < TT:
                            copy_y(t)
                            sum_of_squares(t)
                        if t:
                            silu_tanh(t - 1)
                    return
                for i in range(STEPS):
                    if is_first(b):
                        c = stored_chunk(b, i)
                        evac(i, 0)
                        evac(i, 2)
                        if i == 0:
                            action_again(0)
                        if c is not None:
                            store_gate_up(c, aux)
                        if valued_chunk(b, i) is not None:
                            biased_codes(valued_chunk(b, i))
                        if c is not None:
                            store_down(c, aux)
                        evac(i, 4)
                        if i:
                            hidden_high(i)
                            hidden_bfloat(i)
                        gate_tanh(i)
                        evac(i, 6)
                        aux_read(2 * i)
                        aux_read(2 * i + 1)
                        continue
                    evac(i, 0)
                    if prev and i == 2:
                        copy_y(2)
                        copy_y(3)
                    aux_read(2 * i)
                    evac(i, 2)
                    if prev:
                        if i == 1:
                            copy_y(0)
                        if i in (3, 4, 5):
                            sum_of_squares(i - 2)
                    evac(i, 4)
                    if i or prev:
                        hidden_high(i)
                    aux_read(2 * i + 1)
                    evac(i, 6)
                    gate_tanh(i)
                    if prev:
                        if i == 1:
                            copy_y(1)
                        if i == 2:
                            sum_of_squares(0)
                        if i in TANH_STEPS:
                            silu_tanh(TANH_STEPS.index(i))

            run_batches(act, iteration)

        @block.vector
        def _(dve):
            def bn(B, t):
                if is_first(B):
                    dve.wait_ge(x_first[t], 16)
                else:
                    dve.wait_ge(xin_loaded, 16 * B)
                wait(dve, aggr_done, 4 * B)
                nc.vector.bn_stats(stats[:, t, :], xn[:, t, :]).then_inc(bn_done, 1)

            def stats_complete(B):
                dve.wait_ge(bn_done, 4 * B + 4)
                wait(dve, xn_done, 4 * B)
                wait(dve, var_done, B)

            def aggregate(B):
                for t in range(TT):
                    nc.vector.bn_aggr(mv[:, t, :], stats[:, t, :]).then_inc(aggr_done, 1)

            def norm(B, t):
                if t == 0:
                    dve.wait_ge(rstd_done, B + 1)
                    dve.wait_ge(aggr_done, 4 * B + 4)
                nc.vector.tensor_scalar(xn[:, t, :], xn[:, t, :], mv[:, t, 0:1], rstd[:, t:t + 1], ALU.subtract,
                                        ALU.mult).then_inc(xn_done, 1)

            def xt_low(B, par, k, bank):
                dve.wait_ge(xthi_done, 8 * B + 2 * k + 1)
                nc.vector.tensor_tensor(xt_lo[:, k, :], bank[:, :], xt_hi[:, k, :].bitcast(F32), ALU.subtract)\
                    .then_inc(xtlo_done, 1)
                dve.wait_ge(xthi_done, 8 * B + 2 * k + 2)
                nc.vector.scalar_tensor_tensor(x16[:, par, 1, k, :], bank[:, :], XSCALE, x16[:, par, 0, k, :],
                                               ALU.mult, ALU.subtract).then_inc(xtlo_done, 1)

            links = [0]

            def link(instruction):
                links[0] += 1
                instruction.then_inc(dq, 1)
                dve.wait_ge(dq, links[0])

            def chunk_parts(c):
                gu = pk_gu.rearrange("p (t s) w -> p t s w", t=2)[:, :, c, :].bitcast(U16)
                down = pk_d[:, :, 16 * c:16 * c + 16].bitcast(U16)
                to_gu = mag16[:, 0:8 * P].rearrange("p (t w k) -> p t w k", t=2, k=4)
                to_down = mag16[:, 8 * P:12 * P].rearrange("p (t w k) -> p t w k", t=KT, k=4)
                return (gu, to_gu), (down, to_down)

            def magnitude_codes(c):
                if c:
                    dve.wait_ge(value_ready, c)
                for src, dst in chunk_parts(c):
                    for k in range(4):
                        last = nc.vector.tensor_scalar(dst[:, :, :, k], src, 4 * k, 7, ALU.logical_shift_right,
                                                       ALU.bitwise_and)
                last.then_inc(codes, 1)

            def magnitudes(c):
                dve.wait_ge(codes, c + 1)
                dve.wait_ge(biased, c + 1)
                link(nc.vector.tensor_scalar(mag16, mag16, float(0x3800), float(0x7000), ALU.mult, ALU.min))
                nc.vector.tensor_tensor(value16, mag16, value16, ALU.min).then_inc(dq, 1)
                links[0] += 1

            def sign_bits(c):
                dve.wait_ge(dq, links[0])
                for src, dst in chunk_parts(c):
                    for k in range(4):
                        last = nc.vector.tensor_scalar(dst[:, :, :, k], src, 12 - 4 * k, 0x8000,
                                                       ALU.logical_shift_left, ALU.bitwise_and)
                links[0] += 1
                last.then_inc(dq, 1)

            def signed_values(c):
                dve.wait_ge(dq, links[0])
                value32 = value16.bitcast(U32)
                nc.vector.tensor_tensor(value32, value32, mag[:, :], ALU.bitwise_or).then_inc(value_ready, 1)

            def down_low(c, bank):
                dve.wait_ge(dhi_done, c + 1)
                nc.vector.tensor_tensor(wd_lo[:, c, :], bank[:, :], wd_hi[:, c, :].bitcast(F32), ALU.subtract)\
                    .then_inc(dlo_done, 1)

            for t in range(TT):
                bn(0, t)
            stats_complete(0)
            aggregate(0)
            dve.wait_ge(d_ahead, 48)
            magnitude_codes(0)
            for t in range(TT):
                norm(0, t)
            magnitudes(0)
            sign_bits(0)
            signed_values(0)
            dve.wait_ge(scale_fill, 2)
            nc.vector.tensor_copy(sc_d[:, :, :],
                                  ring[1][:, 0:KT * 16].rearrange("p (k g) -> p k g", g=16)[:, :, 0:STEPS])\
                .then_inc(scale_done, 1)
            raw = ring[0][:, :].bitcast(F16)[:, 0:2 * STEPS * KT].rearrange("p (t k) -> p t k", k=KT)
            nc.vector.tensor_scalar(sc_gu[:, 0:STEPS, :], raw[:, 0:STEPS, :], 1.0 / XSCALE, None, ALU.mult)
            nc.vector.tensor_scalar(sc_gu[:, STEPS:2 * STEPS, :], raw[:, STEPS:2 * STEPS, :], 0.5 / XSCALE, None,
                                    ALU.mult).then_inc(scale_done, 1)
            for k in range(KT):
                xt_low(0, 0, k, x0_bank[k])
            magnitude_codes(1)
            down_low(0, aux)
            magnitudes(1)
            sign_bits(1)
            signed_values(1)
            dve.wait_ge(d_gu, 32)
            dve.wait_ge(d_down, 16)

            def state_action_low(B, bank):
                dve.wait_ge(sa_hi, 2 * B + 2)
                nc.vector.tensor_tensor(state[RANK:2 * RANK, :], bank[0:RANK, :], state[0:RANK, :].bitcast(F32),
                                        ALU.subtract).then_inc(sa_lo, 1)
                nc.vector.tensor_tensor(a_lo[:, :], bank[RANK:2 * RANK, :], action[0:RANK, :].bitcast(F32),
                                        ALU.subtract).then_inc(sa_lo, 1)

            state_action_low(0, ring[2])

            def wo_low(k):
                dve.wait_ge(wohi_done, k + 1)
                nc.vector.tensor_tensor(wo_lo[:, k, :], wo_bank[k][:, :], wo_hi[:, k, :].bitcast(F32),
                                        ALU.subtract).then_inc(wolo_done, 1)

            def iteration(b, par, work, prev, more):
                def evac(i, u):
                    sp = (par + i) % 2
                    dve.wait_ge(act_evac, NU // 2 * b + KT * i + u // 2 + 1)
                    dve.wait_ge(unit_done, NU * b + UNITS * i + u + 1)
                    dst = acc[:, {1: sp, 3: 4, 5: 2 + sp, 7: 5}[u], :]
                    t = i if u < KT else STEPS + i
                    nc.vector.scalar_tensor_tensor(dst, ring[SLOTS_OF[UNITS * i + u]][:, :],
                                                   sc_gu[:, t, u % KT:u % KT + 1], dst, ALU.mult, ALU.add)\
                        .then_inc(dve_evac, 1)

                def hidden(i):
                    dst = acc[:, 2 + (par + i - 1) % 2, :]
                    dve.wait_ge(m_done, STEPS * b + i)
                    dve.wait_ge(tanh_done, STEPS * b + i)
                    nc.vector.scalar_tensor_tensor(dst, th[:, :], 1.0, dst, ALU.add, ALU.mult).then_inc(h_done, 1)
                    if is_first(b):
                        return
                    dve.wait_ge(h_done, STEPS * b + i)
                    wait(dve, down_done, 44 * b + 4 * i - 8)
                    nc.vector.tensor_copy(h_bf[:, h_slot(i - 1), :], dst).then_inc(hbf_done, 1)

                def aux_read(index):
                    slot = aux_slot(index, b, more)
                    if slot is None:
                        return
                    kind, n = slot
                    if kind == "T":
                        xt_low(b + 1, 1 - par, n, aux)
                    elif kind == "SA":
                        state_action_low(b, aux)
                    elif kind == "V":
                        dve.wait_ge(vhi_done, 4 * b + n + 1)
                        nc.vector.tensor_tensor(v_lo[:, n, :], aux[:, :], v_hi[:, n, :].bitcast(F32), ALU.subtract)\
                            .then_inc(vlo_done, 1)
                    elif kind == "E":
                        dve.wait_ge(ready[kind], 4 * b + n + 1)
                        nc.vector.reduce_max(smax[:, n:n + 1], aux[:, 0:(n + 1) * P], AX.X).then_inc(max_done, 1)
                        dve.wait_ge(max_done, 4 * b + n + 1)
                        nc.vector.tensor_scalar(nbias[:, n:n + 1], smax[:, n:n + 1], -QSCALE, None, ALU.mult)\
                            .then_inc(nb_done, 1)
                    elif kind == "F":
                        dve.wait_ge(pthi_done, 4 * b + n + 1)
                        cols = (n + 1) * P
                        nc.vector.tensor_tensor(pt_lo[:, 0:cols], aux[:, 0:cols], pt_hi[:, 0:cols].bitcast(F32),
                                                ALU.subtract).then_inc(ptlo_done, 1)
                    else:
                        dve.wait_ge(exp_done, 4 * b + n + 1)
                        nc.vector.reciprocal(rinv[:, n:n + 1], rsum[:, n:n + 1]).then_inc(rinv_done, 1)
                        dve.wait_ge(rinv_done, 4 * b + n + 1)
                        dve.wait_ge(ready[kind], 4 * b + n + 1)
                        wait(dve, fa_done, 4 * (b - 1) + n + 1)
                        nc.vector.scalar_tensor_tensor(att[:, n, :], aux[:, :], rinv[:, n:n + 1], bias[:, :],
                                                       ALU.mult, ALU.add).then_inc(att_done, 1)

                def layer_norm_part(i):
                    if 1 <= i < 1 + TT:
                        bn(b + 1, i - 1)
                    if i == 1 + TT:
                        stats_complete(b + 1)
                        aggregate(b + 1)
                    if i == 2 + TT:
                        for t in range(TT):
                            norm(b + 1, t)

                def gated_half(t):
                    k = 4 * (b - 1) + t
                    dst = fin[:, t, :]
                    dve.wait_ge(ytanh_done, k + 1)
                    nc.vector.scalar_tensor_tensor(dst, dst, r2[:, t:t + 1], att[:, t, :], ALU.mult,
                                                   ALU.mult).then_inc(fa_done, 1)

                def gated(t):
                    k = 4 * (b - 1) + t
                    dst = fin[:, t, :]
                    dve.wait_ge(fa_done, k + 1)
                    nc.vector.scalar_tensor_tensor(dst, fin[:, 6, :], 1.0, dst, ALU.add, ALU.mult)\
                        .then_inc(fb_done, 1)

                if not work:
                    hidden(0)
                    for t in range(TT):
                        gated_half(t)
                        gated(t)
                        k = 4 * (b - 1) + t
                        dve.wait_ge(fb_done, k + 1)
                        dve.wait_ge(xr_loaded[t % 2], 16 * (2 * (b - 1) + t // 2 + 1))
                        nc.vector.tensor_tensor(fin[:, t, :], fin[:, t, :], fin[:, 4 + t % 2, :], ALU.add)\
                            .then_inc(add_done, 1)
                    return
                for i in range(STEPS):
                    if is_first(b):
                        c = valued_chunk(b, i)
                        evac(i, 1)
                        if i == 0:
                            wo_low(0)
                            wo_low(1)
                        if c is not None:
                            magnitude_codes(c)
                        layer_norm_part(i)
                        evac(i, 3)
                        if i == 0:
                            wo_low(2)
                            wo_low(3)
                        if i:
                            hidden(i)
                        if stored_chunk(b, i) is not None:
                            down_low(stored_chunk(b, i), aux)
                        evac(i, 5)
                        if c is not None:
                            magnitudes(c)
                        aux_read(2 * i)
                        evac(i, 7)
                        if c is not None:
                            sign_bits(c)
                        aux_read(2 * i + 1)
                        if c is not None:
                            signed_values(c)
                        continue
                    evac(i, 1)
                    aux_read(2 * i)
                    if prev and i in GATED_STEPS:
                        gated(GATED_STEPS.index(i))
                    if more and i in (6, 7):
                        norm(b + 1, i - 4)
                    evac(i, 3)
                    if i or prev:
                        hidden(i)
                    scores = aux_slot(2 * i + 1, b, more) in (("E", 1), ("E", 3))
                    if scores:
                        aux_read(2 * i + 1)
                    evac(i, 5)
                    if not scores:
                        aux_read(2 * i + 1)
                    if more and i == 3:
                        stats_complete(b + 1)
                    evac(i, 7)
                    if more:
                        if i in (1, 2):
                            bn(b + 1, 2 * i - 2)
                            bn(b + 1, 2 * i - 1)
                        if i == 3:
                            aggregate(b + 1)
                        if i == 5:
                            norm(b + 1, 0)
                            norm(b + 1, 1)
                    if prev and i in TANH_STEPS:
                        gated_half(TANH_STEPS.index(i))

            dve.wait_ge(d_bo, 16)
            run_batches(dve, iteration)

        @block.gpsimd
        def _(pool):
            nc.gpsimd.memset(ident[:, :], 0.0)
            nc.gpsimd.memset(ident16[:, :], 0.0)
            nc.gpsimd.memset(identb[:, :], 0.0)
            nc.gpsimd.memset(maskb[:, :], 0.0)
            for n, value in enumerate(CONSTS):
                last = nc.gpsimd.memset(const[:, n, :], value)
            last.then_inc(const_made, 1)
            pool.wait_ge(const_made, 1)
            for m in (ident, ident16, identb):
                nc.gpsimd.affine_select(out=m[:, :], in_=m[:, :], compare_op=ALU.not_equal, fill=1.0, base=0,
                                        pattern=[[-1, P]], channel_multiplier=1).then_inc(const_made, 1)
            nc.gpsimd.affine_select(out=maskb[:, :], in_=maskb[:, :], compare_op=ALU.is_ge, fill=NEG, base=0,
                                    pattern=[[-1, P]], channel_multiplier=1).then_inc(const_made, 1)

            def rstd_of(B):
                pool.wait_ge(aggr_done, 4 * B + 4)
                wait(pool, xn_done, 4 * B)
                nc.gpsimd.tensor_tensor(vare[:, :], mv[:, :, 1], const[:, 1, :], ALU.add)\
                    .then_inc(var_done, 1)
                pool.wait_ge(var_done, B + 1)
                nc.gpsimd.tensor_tensor(rstd[:, :], vare[:, :], const[:, 0, :], ALU.pow).then_inc(rstd_done, 1)

            def scaled_down(c):
                pool.wait_ge(value_ready, c + 1)
                if c:
                    pool.wait_ge(d_fill, c)
                nc.gpsimd.tensor_tensor(w32.rearrange("p (k n) -> p k n", n=P),
                                        value16.bitcast(F16)[:, 8 * P:12 * P].rearrange("p (k n) -> p k n", n=P),
                                        sc_d[:, :, c].unsqueeze(2).broadcast_to([P, KT, P]), ALU.mult)\
                    .then_inc(w32_ready, 1)

            rstd_of(0)
            pool.wait_ge(scale_done, 1)
            scaled_down(0)
            pool.wait_ge(wsa_split, 1)
            nc.gpsimd.tensor_tensor(wsa_lo[:, :, :], wsa32, wsa_hi[:, :, :].bitcast(F32), ALU.subtract)\
                .then_inc(wsa_done, 1)

            def iteration(b, par, work, prev, more):
                def gate_sum(i):
                    pool.wait_ge(dve_evac, NU // 2 * b + KT * i + 2)
                    dst = acc[:, (par + i) % 2, :]
                    nc.gpsimd.tensor_tensor(dst, dst, acc[:, 4, :], ALU.add).then_inc(gsum, 1)

                def up_sum_and_product(i):
                    G = STEPS * b + i
                    sp = (par + i - 1) % 2
                    dst = acc[:, 2 + sp, :]
                    pool.wait_ge(dve_evac, NU // 2 * b + KT * i)
                    nc.gpsimd.tensor_tensor(dst, dst, acc[:, 5, :], ALU.add).then_inc(usum, 1)
                    pool.wait_ge(usum, G)
                    nc.gpsimd.tensor_tensor(dst, dst, acc[:, sp, :], ALU.mult).then_inc(m_done, 1)

                def hidden_low(i):
                    pool.wait_ge(hhi_done, STEPS * b + i)
                    s = h_slot(i - 1)
                    nc.gpsimd.tensor_tensor(h_lo[:, s, :], acc[:, 2 + (par + i - 1) % 2, :],
                                            h_hi[:, s, :].bitcast(F32), ALU.subtract).then_inc(hlo_done, 1)

                def rms(t):
                    k = 4 * (b - 1) + t
                    pool.wait_ge(sq_done, k + 1)
                    nc.gpsimd.tensor_tensor(msq[:, 0, t:t + 1], ssq[:, t:t + 1], const[:, 2, 0:1], ALU.mult)\
                        .then_inc(msq_done, 1)
                    pool.wait_ge(msq_done, 2 * k + 1)
                    nc.gpsimd.tensor_tensor(msq[:, 1, t:t + 1], msq[:, 0, t:t + 1], const[:, 3, 0:1], ALU.add)\
                        .then_inc(msq_done, 1)
                    pool.wait_ge(msq_done, 2 * k + 2)
                    nc.gpsimd.tensor_tensor(r2[:, t:t + 1], msq[:, 1, t:t + 1], const[:, 0, 0:1], ALU.pow)\
                        .then_inc(r2_done, 1)

                def add_x(t):
                    k = 4 * (b - 1) + t
                    pool.wait_ge(fb_done, k + 1)
                    pool.wait_ge(xr_loaded[t % 2], 16 * (2 * (b - 1) + t // 2 + 1))
                    dst = fin[:, t, :]
                    nc.gpsimd.tensor_tensor(dst, dst, fin[:, 4 + t % 2, :], ALU.add).then_inc(add_done, 1)

                if not work:
                    up_sum_and_product(0)
                    hidden_low(0)
                    for t in range(TT):
                        rms(t)
                    return
                for i in range(STEPS):
                    if i or prev:
                        up_sum_and_product(i)
                    if stored_chunk(b, i) is not None:
                        scaled_down(stored_chunk(b, i))
                    if is_first(b) and i == 6:
                        rstd_of(b + 1)
                    gate_sum(i)
                    if prev and i in (3, 4):
                        rms(i - 3)
                    if i or prev:
                        hidden_low(i)
                    if prev and i in (5, 7):
                        rms(2 if i == 5 else 3)
                    if prev and i in ADD_X_STEPS:
                        add_x(ADD_X_STEPS.index(i))
                    if more and not is_first(b) and i == 4:
                        rstd_of(b + 1)

            run_batches(pool, iteration)


_INS = ['L0_attn_x', 'L0_attn_Ws', 'L0_attn_Wa', 'L0_attn_Wo', 'L0_attn_bo', 'L0_ffn_gate_up_packed',
        'L0_ffn_gate_up_scales', 'L0_ffn_down_packed', 'L0_ffn_down_scales']


def kernel(**inputs):
    import numpy as _np
    import concourse.bacc as _bacc
    from concourse import mybir as _mybir
    from concourse.bass_utils import run_bass_kernel_spmd as _run

    nc = _bacc.Bacc("TRN2", target_bir_lowering=False, num_devices=1)
    arrays, args = {}, []
    for name in _INS:
        a = _np.ascontiguousarray(inputs[name])
        arrays[f"in_{name}_dram"] = a
        args.append(nc.dram_tensor(f"in_{name}_dram", a.shape, _mybir.dt.from_np(a.dtype), kind="ExternalInput").ap())
    shape = arrays["in_L0_attn_x_dram"].shape
    out = nc.dram_tensor("out_0_dram", shape, _mybir.dt.from_np(_np.dtype("float32")), kind="ExternalOutput").ap()
    gated_attention_ffn(nc, *args, out)
    r = _run(nc, [arrays], core_ids=[0])
    return r.results[0]["out_0_dram"]
```
